# Optimizing a Trainium2 kernel written in Bass

```python
import numpy as np
import jax
import jax.numpy as jnp

def _softmax(x, axis=-1):
    return jax.nn.softmax(x, axis=axis)

def _gelu(x):
    return jax.nn.gelu(x, approximate=True)

def _silu(x):
    return jax.nn.silu(x)

def _sigmoid(x):
    return jax.nn.sigmoid(x)

def _layernorm(x, axis=-1, eps=1e-05):
    m = jnp.mean(x, axis=axis, keepdims=True)
    v = jnp.var(x, axis=axis, keepdims=True)
    return (x - m) / jnp.sqrt(v + eps)

def _scatter_add(tgt, idx, src, axis=0):
    return tgt.at[idx].add(src)

def _segment_sum(src, seg, n):
    return jax.ops.segment_sum(src, seg, n)
kernel_name = 'mk_seq_postln_d1_jaxref_r8_615207'

def setup_inputs(seed: int=0):
    np.random.seed(seed)
    _w = jnp.asarray

    def _L0_attn_setup():
        import jax, jax.numpy as jnp
        import numpy as np
        from jax import lax
        D_MODEL = 128
        N_HEADS = 8
        D_HEAD = 64
        D_INNER = N_HEADS * D_HEAD
        B, T = (4, 512)
        LN_EPS = 1e-05
        NORM_EPS = 1e-12
        key = jax.random.key(seed)
        ks = jax.random.split(key, 6)
        s_proj = (2.0 / (D_MODEL + D_INNER)) ** 0.5
        x = jax.random.normal(ks[0], (B, T, D_MODEL), jnp.float32)
        Wq = jax.random.normal(ks[1], (D_MODEL, D_INNER), jnp.float32) * s_proj
        Wk = jax.random.normal(ks[2], (D_MODEL, D_INNER), jnp.float32) * s_proj
        Wv = jax.random.normal(ks[3], (D_MODEL, D_INNER), jnp.float32) * s_proj
        Wa = jax.random.normal(ks[4], (D_MODEL, D_INNER), jnp.float32) * s_proj
        ba = jnp.full((D_INNER,), 3.0, jnp.float32)
        Wo = jax.random.normal(ks[5], (D_INNER, D_MODEL), jnp.float32) * s_proj
        gamma = jnp.ones((D_MODEL,), jnp.float32)
        beta = jnp.zeros((D_MODEL,), jnp.float32)
        return {'x': x, 'Wq': Wq, 'Wk': Wk, 'Wv': Wv, 'Wa': Wa, 'ba': ba, 'Wo': Wo, 'gamma': gamma, 'beta': beta}
    _L0_attn_in = _L0_attn_setup()

    def _L0_ffn_setup():
        import jax, jax.numpy as jnp
        import numpy as np
        H = 128
        F = 512
        E = 8
        K = 2
        B, S = (2, 128)
        key = jax.random.key(seed)
        k0, k1, k2, k3, k4 = jax.random.split(key, 5)
        s = 0.02
        x = jax.random.normal(k0, (B, S, H), dtype=jnp.float32)
        Wr = jax.random.normal(k1, (E, H), dtype=jnp.float32) * s
        W1 = jax.random.normal(k2, (E, H, F), dtype=jnp.float32) * s
        W3 = jax.random.normal(k3, (E, H, F), dtype=jnp.float32) * s
        W2 = jax.random.normal(k4, (E, F, H), dtype=jnp.float32) * s
        return {'x': x, 'Wr': Wr, 'W1': W1, 'W2': W2, 'W3': W3}
    _L0_ffn_in = _L0_ffn_setup()
    _d = {'L0_attn_x': _L0_attn_in['x'], 'L0_attn_Wq': _L0_attn_in['Wq'], 'L0_attn_Wk': _L0_attn_in['Wk'], 'L0_attn_Wv': _L0_attn_in['Wv'], 'L0_attn_Wa': _L0_attn_in['Wa'], 'L0_attn_ba': _L0_attn_in['ba'], 'L0_attn_Wo': _L0_attn_in['Wo'], 'L0_attn_gamma': _L0_attn_in['gamma'], 'L0_attn_beta': _L0_attn_in['beta'], 'L0_ffn_Wr': _L0_ffn_in['Wr'], 'L0_ffn_W1': _L0_ffn_in['W1'], 'L0_ffn_W2': _L0_ffn_in['W2'], 'L0_ffn_W3': _L0_ffn_in['W3']}
    _x0 = _d['L0_attn_x']
    _d['L0_attn_x'] = jax.random.normal(jax.random.fold_in(jax.random.key(seed), 1), (16, 256, 128), dtype=_x0.dtype)
    del _x0
    return _d

def reference(L0_attn_x, L0_attn_Wq, L0_attn_Wk, L0_attn_Wv, L0_attn_Wa, L0_attn_ba, L0_attn_Wo, L0_attn_gamma, L0_attn_beta, L0_ffn_Wr, L0_ffn_W1, L0_ffn_W2, L0_ffn_W3):

    def _L0_attn_ref(x, Wq, Wk, Wv, Wa, ba, Wo, gamma, beta):
        import jax, jax.numpy as jnp
        import numpy as np
        from jax import lax
        D_MODEL = 128
        N_HEADS = 8
        D_HEAD = 64
        D_INNER = N_HEADS * D_HEAD
        B, T = (4, 512)
        LN_EPS = 1e-05
        NORM_EPS = 1e-12
        Bx, Tx, _ = x.shape
        residual = x
        mu = jnp.mean(x, axis=-1, keepdims=True)
        var = jnp.var(x, axis=-1, keepdims=True)
        xn = (x - mu) / jnp.sqrt(var + LN_EPS) * gamma + beta

        def heads(y):
            return jnp.moveaxis(y.reshape(Bx, Tx, N_HEADS, D_HEAD), 1, 0)
        q = heads(xn @ Wq)
        k = heads(xn @ Wk)
        v = heads(xn @ Wv)
        alpha = jax.nn.sigmoid(heads(xn @ Wa + ba))
        knorm = jnp.linalg.norm(k, axis=-1, keepdims=True)
        k = k / jnp.maximum(knorm, NORM_EPS)

        def step(S, inp):
            q_t, k_t, v_t, a_t = inp
            S = a_t[..., None] * S + k_t[..., None] * v_t[..., None, :]
            o_t = jnp.einsum('bhji,bhj->bhi', S, q_t)
            return (S, o_t)
        S0 = jnp.zeros((Bx, N_HEADS, D_HEAD, D_HEAD), x.dtype)
        _, outs = lax.scan(step, S0, (q, k, v, alpha))
        out = jnp.moveaxis(outs, 0, 1).reshape(Bx, Tx, D_INNER) @ Wo
        return out + residual

    def _L0_ffn_ref(x, Wr, W1, W2, W3):
        import jax, jax.numpy as jnp
        import numpy as np
        H = 128
        F = 512
        E = 8
        K = 2
        B, S = (2, 128)
        b, s, h = x.shape
        xf = x.reshape(-1, h)
        T = xf.shape[0]
        logits = xf @ Wr.T
        probs = jax.nn.softmax(logits, axis=-1)
        _, idx = jax.lax.top_k(probs, K)
        w = jnp.take_along_axis(probs, idx, axis=-1)
        w = w / w.sum(axis=-1, keepdims=True)
        combine = jnp.zeros((T, E), xf.dtype).at[jnp.arange(T)[:, None], idx].set(w)
        gate = jax.nn.silu(jnp.einsum('th,ehf->tef', xf, W1))
        up = jnp.einsum('th,ehf->tef', xf, W3)
        hmid = gate * up
        out = jnp.einsum('te,tef,efh->th', combine, hmid, W2)
        return out.reshape(b, s, h)
    x = L0_attn_x
    x = _layernorm(x + _L0_attn_ref(x, L0_attn_Wq, L0_attn_Wk, L0_attn_Wv, L0_attn_Wa, L0_attn_ba, L0_attn_Wo, L0_attn_gamma, L0_attn_beta), axis=-1)
    x = _layernorm(x + _L0_ffn_ref(x, L0_ffn_Wr, L0_ffn_W1, L0_ffn_W2, L0_ffn_W3), axis=-1)
    return x

_drawn_inputs = setup_inputs


def setup_inputs(seed=0):
    import zlib

    import numpy as np

    out = dict(_drawn_inputs(seed))
    spreads = {'L0_attn_ba': (3.0, 0.2), 'L0_attn_gamma': (1.0, 0.2), 'L0_attn_beta': (0.0, 0.1)}
    factors = {'L0_ffn_Wr': 7.781, 'L0_ffn_W1': 6.858, 'L0_ffn_W2': 6.834, 'L0_ffn_W3': 6.823}
    for name, (base, spread) in spreads.items():
        noise = np.random.default_rng([zlib.crc32(name.encode()), seed]).standard_normal(out[name].shape)
        drawn = base * np.exp(spread * noise) if base else spread * noise
        out[name] = jnp.asarray(drawn.astype(out[name].dtype))
    for name, factor in factors.items():
        out[name] = (out[name] * factor).astype(out[name].dtype)
    return out
```

```python
import math
from contextlib import ExitStack

import concourse.bass as bass
import concourse.mybir as mybir

P = 128
F32 = mybir.dt.float32
I32 = mybir.dt.int32
U32 = mybir.dt.uint32
ALU = mybir.AluOpType
ACT = mybir.ActivationFunctionType
AXIS = mybir.AxisListType

LN_EPS = 1e-5
NORM_EPS = 1e-12
DECAY_LIMIT = 40.0
SS_SCALE = 2.0 ** 20
GATE_FLOOR = -40.0
SIGMOID_FLOOR = -87.0


def at_least(eng, sem, count):
    if isinstance(count, int) and count <= 0:
        return
    eng.wait_ge(sem, count)


def build(nc, x, wq, wk, wv, wa, ba_t, wo, gamma, beta, wr_t, w1, w2, w3, out):
    B, T, D = x.shape
    DI = wq.shape[1]
    G = DI // P
    HG = 2
    H = G * HG
    DH = DI // H
    E, _, F = w1.shape
    FC = F // P
    NT = B * T
    TPB = T // P
    NTILES = NT // P
    BLK = 512
    TB = BLK // P
    NBLK = NT // BLK
    GT = G * T

    TOPK = 2
    ROW = D + 2
    PART = NT + P
    EMPTY_ROW = E * PART
    NROWS = EMPTY_ROW + P
    NSLOT = TOPK * NTILES + E
    CONSTS = 14
    TABLE = 19
    EXP_LN_SET = 6

    rows_d = nc.dram_tensor("expert_rows", [NROWS, ROW], F32).ap()
    made_d = nc.dram_tensor("made_rows", [TOPK * NT + NSLOT * P, D], F32).ap()
    x_d = x.rearrange("b t d -> (b t) d").rearrange("(n p) d -> p n d", p=P)
    out_d = out.rearrange("b t d -> (b t) d").rearrange("(n p) d -> p n d", p=P)

    with ExitStack() as ctx:
        def sb(name, shape, dt=F32):
            return ctx.enter_context(nc.sbuf_tensor(name, shape, dt))

        def sem(name):
            return ctx.enter_context(nc.semaphore(name))

        x_sb = sb("x_sb", [P, NTILES, D])
        y_sb = sb("y_sb", [P, NTILES, D])
        xnT = sb("xnT", [P, NT])
        wq_sb = sb("wq_sb", [P, DI])
        wk_sb = sb("wk_sb", [P, DI])
        wv_sb = sb("wv_sb", [P, DI])
        wa_sb = sb("wa_sb", [P, DI])
        wo_sb = sb("wo_sb", [P, G, D])
        w1_sb = sb("w1_sb", [P, E, F])
        w3_sb = sb("w3_sb", [P, E, F])
        w2_sb = sb("w2_sb", [P, E, FC, D])
        wr_sb = sb("wr_sb", [P, E])
        ba_sb = sb("ba_sb", [P, G])
        gamma_sb = sb("gamma_sb", [P, 1])
        beta_sb = sb("beta_sb", [P, 1])
        ident = sb("ident", [P, P])
        causal = sb("causal", [P, 3 * P])
        head_sel = sb("head_sel", [P, G, H])
        keep = sb("keep", [P, G, T])
        eps_sb = sb("eps_sb", [P, 1])
        log_scale = sb("log_scale", [P, 1])
        ones_col = sb("ones_col", [P, 1])
        iota8 = sb("iota8", [P, E])
        iota_i = sb("iota_i", [P, E], I32)
        earlier = sb("earlier", [P, P])
        all_ones = sb("all_ones", [P, P])
        first_row = sb("first_row", [P, E])
        next_row = sb("next_row", [P, E])
        made_i = sb("made_i", [P, TOPK * NTILES + 1], I32)
        made_to = sb("made_to", [P, TOPK, NTILES])
        lane_f = sb("lane_f", [P, 1])
        expert_no = sb("expert_no", [P, E])
        ones8 = sb("ones8", [P, E])
        tile_no = sb("tile_no", [P, NSLOT])
        tile_edge = sb("tile_edge", [P, NSLOT])
        table_i = sb("table_i", [P, NSLOT], I32)
        lane_i = sb("lane_i", [P, 1], I32)
        empty = sb("empty", [P, ROW])
        pad_i = sb("pad_i", [P, E], I32)
        count, ntile, tiles_to, tiles_from = (sb(n, [P, E]) for n in ("count", "ntile", "tiles_to", "tiles_from"))
        full = sb("full", [P, E, NTILES])
        mine, work = sb("mine", [P, NSLOT, E]), sb("work", [P, NSLOT, E])
        slot_tab = sb("slot_tab", [P, NSLOT])
        expert_i, row_i = sb("expert_i", [P, NSLOT], I32), sb("row_i", [P, NSLOT], I32)
        rng_sb = sb("rng_sb", [P, B, G, 2])
        flag_f = sb("flag_f", [P, 1])
        flag_i = sb("flag_i", [P, 1], I32)

        s_x = [sem(f"x_loaded{n}") for n in range(4)]
        s_affine = sem("gamma_beta_bias_loaded")
        s_wa, s_wq, s_wk, s_wv, s_wo, s_wr = (sem(n + "_loaded") for n in ("wa", "wq", "wk", "wv", "wo", "wr"))
        s_wm = sem("expert_weights_loaded")
        s_id0 = sem("ident_zeroed")
        s_id = sem("ident_ready")
        s_const0 = sem("constants_filled")
        s_const = sem("constants_ready")
        s_iota = sem("iota_written")
        s_fill, s_pads, s_turn = sem("empty_rows_filled"), sem("empty_tiles_sent"), sem("pool_turn")
        s_sent = sem("rows_sent")
        m_first, m_pad, m_table = sem("m_first"), sem("m_pad"), sem("m_table")
        s_bn = sem("ln0_stats")
        s_ag = sem("ln0_aggregated")
        s_rs = sem("ln0_rstd")
        s_xh = sem("ln0_normalised")
        s_xt = sem("ln0_transposed")
        s_xn = sem("xnT_written")
        z_ready, q_ready, k_ready = sem("z_ready"), sem("q_ready"), sem("k_ready")
        v_ready, ss_ready = sem("v_ready"), sem("ss_ready")
        at_ready, av_done, o_ready, y_ready = sem("at_ready"), sem("av_done"), sem("o_ready"), sem("y_ready")
        z_done = sem("z_done")
        e_done, sp_done, sq_done = sem("e_done"), sem("sp_done"), sem("sq_done")
        eq_done, ek_done, o_copied = sem("eq_done"), sem("ek_done"), sem("o_copied")
        l_done, qd_done, kd_done = sem("l_done"), sem("qd_done"), sem("kd_done")
        masked, rn_done, vs_done = sem("masked"), sem("rn_done"), sem("vs_done")
        ss_done = sem("ss_done")
        y_done, rng_done = sem("y_done"), sem("rng_done")
        xs_done, lc_raw, lc_done = sem("xs_done"), sem("lc_raw"), sem("lc_done")
        s_fl = sem("flag_steps")
        s_flag_sum = sem("flag_sum")
        s_flag = sem("flag_ready")

        def load_table(number):
            nc.scalar.add_instruction(mybir.InstLoadActFuncSet(
                act_func_set_id=number, name=nc.get_next_instruction_name(),
                engine=mybir.EngineType.Activation, ins=[], outs=[]))

        def join_halves(dve, st, mean, var, tmp, done, base):
            nc.vector.tensor_tensor(mean[:], st[:, :, 1], st[:, :, 4], ALU.add).then_inc(done, 1)
            nc.vector.tensor_tensor(tmp[:], st[:, :, 1], st[:, :, 4], ALU.subtract).then_inc(done, 1)
            nc.vector.tensor_tensor(var[:], st[:, :, 2], st[:, :, 5], ALU.add).then_inc(done, 1)
            dve.wait_ge(done, base + 3)
            nc.vector.tensor_scalar(mean[:], mean[:], 0.5, None, ALU.mult).then_inc(done, 1)
            nc.vector.scalar_tensor_tensor(tmp[:], tmp[:], 0.25, tmp[:], ALU.mult, ALU.mult).then_inc(done, 1)
            dve.wait_ge(done, base + 5)
            nc.vector.scalar_tensor_tensor(var[:], var[:], 1.0 / D, tmp[:], ALU.mult, ALU.add).then_inc(done, 1)

        with nc.Block() as block, ExitStack() as c1:
            def sb1(name, shape):
                return c1.enter_context(nc.sbuf_tensor(name, shape, F32))

            def ps1(name, shape):
                return c1.enter_context(nc.psum_tensor(name, shape, F32))

            xs = sb1("xs", [P, 2, T])
            sp = sb1("sp", [P, G, T])
            lsum = sb1("lsum", [P, G, T])
            lc = sb1("lc", [P, G, T])
            eq = sb1("eq", [P, G, T])
            ek = sb1("ek", [P, G, T])
            k2 = sb1("k2", [P, G, T])
            qd = sb1("qd", [P, 2, G, T])
            kd = sb1("kd", [P, 2, G, T])
            vs = sb1("vs", [P, 2, TPB, DI])
            ss = sb1("ss", [P, TPB, H])
            rn = sb1("rn", [P, TPB, H])
            am = sb1("am", [P, 4, 3 * P])
            ob = sb1("ob", [P, G, T])
            NX = 4
            XT, BPX = NTILES // NX, NBLK // NX
            st0 = sb1("st0", [P, NTILES, 6])
            mean0, var0, rs0, tmp0 = (sb1(n, [P, NTILES]) for n in ("mean0", "var0", "rs0", "tmp0"))
            pA = ps1("pA", [P, G, T])
            pB = ps1("pB", [P, G * T])
            pAT = [ps1(f"pAT{i}", [P, 512]) for i in range(2)]
            pO = [ps1(f"pO{i}", [P, HG, T]) for i in range(2)]
            turned = [pO[a][:].rearrange("p h t -> p (h t)") for a in range(BPX)]
            pV = pB[:, :].rearrange("p (n c) -> p n c", n=TPB)
            pQ = pB[:, :].rearrange("p (g t) -> p g t", g=G)
            pSS = pAT[1][:, 0:TPB * H].rearrange("p (n h) -> p n h", n=TPB)
            pY = pAT[0][:, 0:TPB * D].rearrange("p (n d) -> p n d", n=TPB)

            def rows(loop_engine, step):
                step(0, 0)
                step(1, 1)
                with loop_engine.Fori(1, B // 2 - 1) as j:
                    step(2 * j, 0)
                    step(2 * j + 1, 1)
                step(B - 2, 0)
                step(B - 1, 1)

            def of_part(n):
                return slice(n * XT, (n + 1) * XT)

            def is_last(i):
                return isinstance(i, int) and i == B - 1

            @block.sync
            def _(sync):
                for n in range(NX):
                    sync.dma_start(x_sb[:, of_part(n), :], x_d[:, of_part(n), :]).then_inc(s_x[n], 16)
                sync.dma_start(wv_sb[:], wv).then_inc(s_wv, 16)
                sync.dma_start(wo_sb[:], wo.rearrange("(g p) d -> p g d", p=P)).then_inc(s_wo, 16)
                sync.dma_start(wr_sb[:], wr_t).then_inc(s_wr, 16)
                sync.dma_start(w1_sb[:], w1.rearrange("e h f -> h e f")).then_inc(s_wm, 16)
                sync.dma_start(w2_sb[:], w2.rearrange("e (c p) h -> p e c h", p=P)).then_inc(s_wm, 16)

            @block.tensor
            def _(pe):
                def turn_x(n):
                    for a in range(BPX):
                        blk = n * BPX + a
                        pe.wait_ge(s_xh, TB * (blk + 1))
                        at_least(pe, s_xn, blk - BPX + 1)
                        for t in range(TB):
                            mm = nc.tensor.transpose(turned[a][:, t * P:(t + 1) * P], y_sb[:, blk * TB + t, :], ident[:])
                        mm.then_inc(s_xt, 1)

                def project(dst, w, b):
                    for g in range(G):
                        mm = nc.tensor.matmul(dst[:, g, :], w[:, g * P:(g + 1) * P], xnT[:, bass.ds(b * T, T)],
                                              start=True, stop=True)
                    return mm

                def gates(b):
                    at_least(pe, kd_done, b)
                    project(pA, wa_sb, b).then_inc(z_ready, 1)

                def queries(b):
                    at_least(pe, vs_done, b)
                    project(pQ, wq_sb, b).then_inc(q_ready, 1)

                def keys(b):
                    pe.wait_ge(z_done, G * (b + 1))
                    project(pA, wk_sb, b).then_inc(k_ready, 1)

                def v_norms(b, p):
                    pe.wait_ge(qd_done, b + 1)
                    pe.wait_ge(xs_done, b + 1)
                    for n in range(TPB):
                        mm = nc.tensor.matmul(pV[:, n, :], xs[:, p, n * P:(n + 1) * P], wv_sb[:],
                                              start=True, stop=True)
                    mm.then_inc(v_ready, 1)
                    pe.wait_ge(sq_done, b + 1)
                    at_least(pe, masked, H * b)
                    for n in range(TPB):
                        for g in range(G):
                            mm = nc.tensor.matmul(pSS[:, n, :], k2[:, g, n * P:(n + 1) * P], head_sel[:, g, :],
                                                  start=g == 0, stop=g == G - 1)
                    mm.then_inc(ss_ready, 1)

                def scores(b, p, h):
                    if h == 0:
                        pe.wait_ge(kd_done, b + 1)
                        pe.wait_ge(qd_done, b + 1)
                        at_least(pe, y_done, b)
                    elif h == 1:
                        pe.wait_ge(ss_done, b + 1)
                    else:
                        pe.wait_ge(masked, H * b + h - 1)
                    g, r = h // HG, slice(DH * (h % HG), DH * (h % HG) + DH)
                    at = pAT[h % 2]
                    nc.tensor.matmul(at[:, 0:T], kd[r, p, g, 0:P], qd[r, p, g, :], start=True, stop=True)
                    nc.tensor.matmul(at[:, T:T + P], kd[r, p, g, P:T], qd[r, p, g, P:T],
                                     start=True, stop=True).then_inc(at_ready, 1)

                def values(b, p, h):
                    if h == 0:
                        pe.wait_ge(vs_done, b + 1)
                        at_least(pe, o_copied, 2 * b - 1)
                    if h == H // 2:
                        at_least(pe, o_copied, 2 * b)
                    pe.wait_ge(masked, H * b + h + 1)
                    g, r = h // HG, slice(DH * (h % HG), DH * (h % HG) + DH)
                    o = pO[g // 2][r, g % 2, :]
                    nc.tensor.matmul(o, vs[:, p, 0, h * DH:(h + 1) * DH], am[:, h % 4, 0:T],
                                     start=True, stop=False, skip_group_check=True)
                    mm = nc.tensor.matmul(o[:, P:T], vs[:, p, 1, h * DH:(h + 1) * DH], am[:, h % 4, T:T + P],
                                          start=False, stop=True, skip_group_check=True)
                    mm.then_inc(av_done, 1)

                def project_out(b):
                    pe.wait_ge(o_copied, 2 * b + 2)
                    pe.wait_ge(masked, H * b + H - 1)
                    for n in range(TPB):
                        for g in range(G):
                            mm = nc.tensor.matmul(pY[:, n, :], ob[:, g, n * P:(n + 1) * P], wo_sb[:, g, :],
                                                  start=g == 0, stop=g == G - 1)
                    mm.then_inc(y_ready, 1)

                pe.wait_ge(s_id, 1)
                turn_x(0)
                pe.wait_ge(s_wa, 16)
                pe.wait_ge(s_xn, BPX)
                gates(0)
                turn_x(1)
                pe.wait_ge(s_wq, 16)
                queries(0)
                pe.wait_ge(s_wk, 16)
                keys(0)
                turn_x(2)
                pe.wait_ge(s_const, CONSTS)
                pe.wait_ge(s_wv, 16)
                v_norms(0, 0)
                turn_x(3)
                pe.wait_ge(s_xn, NBLK)
                pe.wait_ge(s_wo, 16)

                def step(i, p):
                    if not is_last(i):
                        gates(i + 1)
                    scores(i, p, 0)
                    scores(i, p, 1)
                    if not is_last(i):
                        queries(i + 1)
                    for h in range(H):
                        values(i, p, h)
                        if h + 2 < H:
                            scores(i, p, h + 2)
                        if h == 0 and not is_last(i):
                            keys(i + 1)
                    if not is_last(i):
                        v_norms(i + 1, 1 - p)
                    project_out(i)

                rows(pe, step)

            @block.scalar
            def _(act):
                act.dma_start(wa_sb[:], wa).then_inc(s_wa, 16)
                act.dma_start(gamma_sb[:], gamma.rearrange("(p a) -> p a", a=1)).then_inc(s_affine, 16)
                act.dma_start(beta_sb[:], beta.rearrange("(p a) -> p a", a=1)).then_inc(s_affine, 16)
                act.dma_start(ba_sb[:], ba_t).then_inc(s_affine, 16)
                act.dma_start(wq_sb[:], wq).then_inc(s_wq, 16)
                act.dma_start(wk_sb[:], wk).then_inc(s_wk, 16)
                act.dma_start(w3_sb[:], w3.rearrange("e h f -> h e f")).then_inc(s_wm, 16)
                load_table(EXP_LN_SET)

                def deviations(n):
                    tl = of_part(n)
                    act.wait_ge(s_ag, 6 * (n + 1))
                    nc.scalar.activation(rs0[:, tl], var0[:, tl], ACT.Ln, bias=eps_sb[:, 0:1]).then_inc(s_rs, 1)
                    act.wait_ge(s_rs, 2 * n + 1)
                    nc.scalar.activation(rs0[:, tl], rs0[:, tl], ACT.Exp, scale=-0.5).then_inc(s_rs, 1)

                def write_xn(n):
                    for a in range(BPX):
                        blk = n * BPX + a
                        act.wait_ge(s_xt, blk + 1)
                        nc.scalar.activation(xnT[:, blk * BLK:(blk + 1) * BLK], turned[a], ACT.Identity,
                                             scale=gamma_sb[:, 0:1], bias=beta_sb[:, 0:1]).then_inc(s_xn, 1)

                def gates(b):
                    act.wait_ge(z_done, G * (b + 1))
                    nc.scalar.activation(sp[:], sp[:], ACT.Exp, scale=-1.0).then_inc(e_done, 1)
                    act.wait_ge(e_done, b + 1)
                    nc.scalar.activation(sp[:], sp[:], ACT.Ln, bias=1.0).then_inc(sp_done, 1)

                def squares(b):
                    act.wait_ge(k_ready, b + 1)
                    at_least(act, ss_ready, b)
                    nc.scalar.activation(k2[:], pA[:], ACT.Square).then_inc(sq_done, 1)

                def decays(b):
                    act.wait_ge(lc_done, b + 1)
                    at_least(act, qd_done, b)
                    nc.scalar.activation(eq[:], lc[:], ACT.Exp, scale=-1.0).then_inc(eq_done, 1)
                    at_least(act, kd_done, b)
                    nc.scalar.activation(ek[:], lc[:], ACT.Exp).then_inc(ek_done, 1)

                def norms(b):
                    act.wait_ge(ss_done, b + 1)
                    at_least(act, vs_done, b)
                    nc.scalar.activation(rn[:], ss[:], ACT.Ln, scale=SS_SCALE).then_inc(rn_done, 1)
                    act.wait_ge(rn_done, 2 * b + 1)
                    nc.scalar.activation(rn[:], rn[:], ACT.Exp, scale=-0.5, bias=log_scale[:, 0:1]).then_inc(rn_done, 1)

                def copy_out(b, j):
                    act.wait_ge(av_done, H * b + 4 * (j + 1))
                    if j == 0:
                        at_least(act, y_ready, b)
                    nc.scalar.copy(ob[:, 2 * j:2 * j + 2, :], pO[j][:]).then_inc(o_copied, 1)

                act.wait_ge(s_id0, 2)
                deviations(0)
                deviations(1)
                act.wait_ge(s_affine, 16 * 3)
                write_xn(0)
                deviations(2)
                write_xn(1)
                gates(0)
                squares(0)
                deviations(3)
                write_xn(2)
                decays(0)
                write_xn(3)
                act.wait_ge(s_const, CONSTS)
                norms(0)

                def step(i, p):
                    if not is_last(i):
                        gates(i + 1)
                        squares(i + 1)
                        decays(i + 1)
                    copy_out(i, 0)
                    copy_out(i, 1)
                    if not is_last(i):
                        norms(i + 1)

                rows(act, step)

            @block.gpsimd
            def _(pool):
                nc.gpsimd.memset(ident[:], 0.0).then_inc(s_id0, 1)
                nc.gpsimd.memset(eps_sb[:], LN_EPS).then_inc(s_id0, 1)
                pool.wait_ge(s_id0, 2)
                nc.gpsimd.affine_select(out=ident[:], in_=ident[:], compare_op=ALU.not_equal, fill=1.0,
                                        base=0, pattern=[[-1, P]], channel_multiplier=1).then_inc(s_id, 1)
                nc.gpsimd.memset(causal[:], 1.0).then_inc(s_const0, 1)
                nc.gpsimd.memset(head_sel[:], 1.0).then_inc(s_const0, 1)
                nc.gpsimd.memset(ones_col[:], 1.0).then_inc(s_const0, 1)
                nc.gpsimd.memset(keep[:], 1.0).then_inc(s_const0, 1)
                nc.gpsimd.memset(log_scale[:], 0.5 * math.log(SS_SCALE)).then_inc(s_const0, 1)
                nc.gpsimd.iota(iota_i[:], pattern=[[1, E]], base=-E, channel_multiplier=0).then_inc(s_iota, 1)
                nc.gpsimd.memset(earlier[:], 1.0).then_inc(s_const0, 1)
                nc.gpsimd.memset(all_ones[:], 1.0).then_inc(s_const0, 1)
                nc.gpsimd.memset(ones8[:], 1.0).then_inc(s_const0, 1)
                nc.gpsimd.memset(empty[:], 0.0).then_inc(s_const0, 1)
                nc.gpsimd.iota(made_i[:], pattern=[[P, TOPK * NTILES + 1]], base=0, channel_multiplier=1).then_inc(s_iota, 1)
                nc.gpsimd.iota(table_i[:], pattern=[[1, NSLOT]], base=0, channel_multiplier=0).then_inc(s_iota, 1)
                nc.gpsimd.iota(lane_i[:], pattern=[[0, 1]], base=0, channel_multiplier=1).then_inc(s_iota, 1)
                pool.wait_ge(s_const0, 9)
                for c in (0, 2):
                    tri = causal[:, c * P:(c + 1) * P]
                    nc.gpsimd.affine_select(out=tri, in_=tri, compare_op=ALU.is_ge, fill=0.0,
                                            base=0, pattern=[[1, P]], channel_multiplier=-1).then_inc(s_const, 1)
                nc.gpsimd.affine_select(out=head_sel[:], in_=head_sel[:], compare_op=ALU.is_ge, fill=0.0,
                                        base=0, pattern=[[P, G], [-DH, H]],
                                        channel_multiplier=1).then_inc(s_const, 1)
                pool.wait_ge(s_const, 3)
                nc.gpsimd.affine_select(out=head_sel[:], in_=head_sel[:], compare_op=ALU.is_ge, fill=0.0,
                                        base=DH - 1, pattern=[[-P, G], [DH, H]],
                                        channel_multiplier=-1).then_inc(s_const, 1)
                nc.gpsimd.memset(keep[:, :, 0:1], 0.0).then_inc(s_const, 1)
                nc.gpsimd.affine_select(out=earlier[:], in_=earlier[:], compare_op=ALU.is_ge, fill=0.0,
                                        base=-1, pattern=[[1, P]], channel_multiplier=-1).then_inc(s_const, 1)
                pool.wait_ge(s_iota, 4)
                nc.gpsimd.tensor_copy(iota8[:], iota_i[:]).then_inc(s_const, 1)
                nc.gpsimd.tensor_copy(tile_no[:], table_i[:]).then_inc(s_const, 1)
                nc.gpsimd.tensor_copy(lane_f[:], lane_i[:]).then_inc(s_const, 1)
                nc.gpsimd.tensor_copy(empty[:, D + 1:D + 2], made_i[:, TOPK * NTILES:TOPK * NTILES + 1]).then_inc(s_const, 1)
                nc.gpsimd.tensor_copy(made_to[:].rearrange("p k n -> p (k n)"), made_i[:, 0:TOPK * NTILES]).then_inc(s_const, 1)
                pool.wait_ge(s_const, 11)
                nc.gpsimd.tensor_scalar(expert_no[:], iota8[:], float(E), None, ALU.add).then_inc(s_const, 1)
                nc.gpsimd.tensor_scalar(tile_edge[:], tile_no[:], float(P), None, ALU.mult).then_inc(s_const, 1)
                pool.wait_ge(s_const, 13)
                nc.gpsimd.tensor_scalar(first_row[:], expert_no[:], float(PART), None, ALU.mult).then_inc(s_const, 1)
                pool.wait_ge(s_const, 14)
                nc.gpsimd.dma_start(rows_d[EMPTY_ROW:NROWS, :], empty[:]).then_inc(s_fill, 16)

                def prepare(b, p):
                    if isinstance(b, int) and b < 2:
                        pool.wait_ge(s_xn, BPX if b == 0 else NBLK)
                    at_least(pool, v_ready, b - 1)
                    nc.gpsimd.tensor_copy(xs[:, p, :], xnT[:, bass.ds(b * T, T)]).then_inc(xs_done, 1)

                rows(pool, prepare)

            @block.vector
            def _(dve):
                flat = "p g t -> p (g t)"

                def statistics(n):
                    tl = of_part(n)
                    dve.wait_ge(s_x[n], 16)
                    for t in range(n * XT, (n + 1) * XT):
                        nc.vector.bn_stats(st0[:, t, :], x_sb[:, t, :]).then_inc(s_bn, 1)
                    dve.wait_ge(s_bn, XT * (n + 1))
                    join_halves(dve, st0[:, tl], mean0[:, tl], var0[:, tl], tmp0[:, tl], s_ag, 6 * n)

                def normalise(n):
                    dve.wait_ge(s_rs, 2 * (n + 1))
                    for t in range(n * XT, (n + 1) * XT):
                        nc.vector.tensor_scalar(y_sb[:, t, :], x_sb[:, t, :], mean0[:, t:t + 1], rs0[:, t:t + 1],
                                                ALU.subtract, ALU.mult).then_inc(s_xh, 1)

                def gate_logits(b, p):
                    dve.wait_ge(z_ready, b + 1)
                    at_least(dve, l_done, b)
                    for g in range(G):
                        nc.vector.tensor_scalar(sp[:, g, :], pA[:, g, :], ba_sb[:, g:g + 1], GATE_FLOOR,
                                                ALU.add, ALU.max).then_inc(z_done, 1)

                def scan(b, p):
                    dve.wait_ge(sp_done, b + 1)
                    at_least(dve, lc_raw, G * b)
                    nc.vector.tensor_tensor_scan(lsum[:].rearrange(flat), keep[:].rearrange(flat),
                                                 sp[:].rearrange(flat), 0.0, ALU.mult, ALU.add).then_inc(l_done, 1)

                def centre(b, p):
                    dve.wait_ge(l_done, b + 1)
                    at_least(dve, ek_done, b)
                    at_least(dve, rng_done, b)
                    for g in range(G):
                        nc.vector.tensor_scalar(lc[:, g, :], lsum[:, g, :], lsum[:, g, P - 1:P], DECAY_LIMIT,
                                                ALU.subtract, ALU.min).then_inc(lc_raw, 1)
                    dve.wait_ge(lc_raw, G * (b + 1))
                    nc.vector.tensor_scalar(lc[:], lc[:], -DECAY_LIMIT, None, ALU.max).then_inc(lc_done, 1)

                def decay_q(b, p):
                    dve.wait_ge(q_ready, b + 1)
                    dve.wait_ge(eq_done, b + 1)
                    at_least(dve, at_ready, H * (b - 1))
                    nc.vector.tensor_tensor(qd[:, p], pQ, eq[:], ALU.mult).then_inc(qd_done, 1)

                def decay_k(b, p):
                    dve.wait_ge(sq_done, b + 1)
                    dve.wait_ge(ek_done, b + 1)
                    nc.vector.tensor_tensor(kd[:, p], pA[:], ek[:], ALU.mult).then_inc(kd_done, 1)

                def note_range(b, p):
                    dve.wait_ge(lc_done, b + 1)
                    nc.vector.tensor_copy(rng_sb[:, bass.ds(b, 1), :, :].rearrange("p a g e -> p (a g) e"),
                                          lc[:, :, 0:T:T - 1]).then_inc(rng_done, 1)

                def scale_v(b, p):
                    dve.wait_ge(ss_ready, b + 1)
                    at_least(dve, rn_done, 2 * b)
                    nc.vector.tensor_scalar(ss[:], pSS, NORM_EPS ** 2, None, ALU.max).then_inc(ss_done, 1)
                    dve.wait_ge(rn_done, 2 * b + 2)
                    dve.wait_ge(v_ready, b + 1)
                    at_least(dve, av_done, H * (b - 1))
                    nc.vector.tensor_tensor(vs[:, p].rearrange("p n (h d) -> p (n h) d", h=H),
                                            pB[:, :].rearrange("p (m d) -> p m d", d=DH),
                                            rn[:].rearrange("p n h -> p (n h)").unsqueeze(2).to_broadcast([P, TPB * H, DH]),
                                            ALU.mult).then_inc(vs_done, 1)

                def mask(b, h):
                    dve.wait_ge(at_ready, H * b + h + 1)
                    at_least(dve, av_done, H * b + h - 3)
                    nc.vector.tensor_tensor(am[:, h % 4, :], pAT[h % 2][:, 0:3 * P], causal[:],
                                            ALU.mult).then_inc(masked, 1)

                def residual(b):
                    dve.wait_ge(y_ready, b + 1)
                    nc.vector.scalar_tensor_tensor(y_sb[:, bass.ds(TPB * b, TPB), :], x_sb[:, bass.ds(TPB * b, TPB), :],
                                                   2.0, pY, ALU.mult, ALU.add).then_inc(y_done, 1)

                def step(i, p):
                    between = {-1: [gate_logits], 1: [scan], 2: [centre],
                               4: [decay_q], 5: [decay_k], 7: [note_range, scale_v]}
                    for h in range(-1, H):
                        if h >= 0:
                            mask(i, h)
                        if not is_last(i):
                            for stage_of_next in between.get(h, []):
                                stage_of_next(i + 1, 1 - p)
                    residual(i)

                statistics(0)
                statistics(1)
                normalise(0)
                statistics(2)
                normalise(1)
                dve.wait_ge(s_affine, 16 * 3)
                gate_logits(0, 0)
                statistics(3)
                dve.wait_ge(s_const, CONSTS)
                scan(0, 0)
                centre(0, 0)
                normalise(2)
                decay_q(0, 0)
                decay_k(0, 0)
                normalise(3)
                note_range(0, 0)
                scale_v(0, 0)
                rows(dve, step)

                dve.wait_ge(rng_done, B)
                nc.vector.tensor_tensor(rng_sb[:], rng_sb[:], rng_sb[:], ALU.mult).then_inc(s_fl, 1)
                dve.wait_ge(s_fl, 1)
                nc.vector.tensor_scalar(rng_sb[:], rng_sb[:], DECAY_LIMIT ** 2, None, ALU.is_lt).then_inc(s_fl, 1)
                dve.wait_ge(s_fl, 2)
                nc.vector.tensor_reduce(flag_f[:, 0:1], rng_sb[:].rearrange("p b g e -> p (b g e)"), AXIS.X,
                                        ALU.min).then_inc(s_fl, 1)

        with nc.Block() as block, ExitStack() as c2:
            pF = c2.enter_context(nc.psum_tensor("pF", [P, 512], F32))

            @block.tensor
            def _(pe):
                pe.wait_ge(s_fl, 3)
                nc.tensor.matmul(pF[0:1, 0:1], flag_f[:, 0:1], ones_col[:], start=True, stop=True).then_inc(s_flag_sum, 1)

            @block.vector
            def _(dve):
                dve.wait_ge(s_flag_sum, 1)
                nc.vector.tensor_copy(flag_i[0:1, :], pF[0:1, 0:1]).then_inc(s_flag, 1)

        with nc.Block() as block, ExitStack() as c3:
            def sb3(name, shape):
                return c3.enter_context(nc.sbuf_tensor(name, shape, F32))

            g_a = sb3("g_a", [P, T])
            g_k2 = sb3("g_k2", [P, T])
            g_q = sb3("g_q", [P, T])
            g_v = sb3("g_v", [P, T])
            g_n = sb3("g_n", [P, T])
            g_k = sb3("g_k", [P, T])
            g_kv, g_s, g_qs = sb3("g_kv", [P, T]), sb3("g_s", [P, T]), sb3("g_qs", [P, T])
            g_o = sb3("g_o", [P, G, T])
            same_head = sb3("same_head", [P, P])
            spread = sb3("spread", [P, HG, DH])
            place = sb3("place", [P, P])
            window = sb3("window", [P, 3 * DH])
            pz, pk, pq, pv, pn, pb, po, py = (c3.enter_context(nc.psum_tensor(f"g_p{n}", [P, 512], F32))
                                              for n in "zkqvnboy")

            g_const, g_proj, g_act, g_ss = sem("g_const"), sem("g_proj"), sem("g_act"), sem("g_ss")
            g_clamped, g_norm, g_in = sem("g_clamped"), sem("g_norm"), sem("g_in")
            g_sel, g_row, g_kv_done, g_s_done = sem("g_sel"), sem("g_row"), sem("g_kv_done"), sem("g_s_done")
            g_qs_done, g_summed, g_out = sem("g_qs_done"), sem("g_summed"), sem("g_out")
            g_y, g_y_done, g_z = sem("g_y"), sem("g_y_done"), sem("g_z")

            def out_of_range(eng):
                eng.wait_ge(s_flag, 1)
                return eng.If(eng.value_load(flag_i[0:1, 0:1]) < P)

            @block.gpsimd
            def _(pool):
                with out_of_range(pool):
                    nc.gpsimd.memset(same_head[:], 0.0).then_inc(g_const, 1)
                    nc.gpsimd.memset(window[:], 0.0).then_inc(g_const, 1)
                    pool.wait_ge(g_const, 2)
                    for hh in range(HG):
                        r = slice(hh * DH, hh * DH + DH)
                        nc.gpsimd.memset(same_head[r, r], 1.0).then_inc(g_const, 1)
                        nc.gpsimd.memset(window[r, DH * (1 + hh):DH * (1 + hh) + 1], 1.0).then_inc(g_const, 1)

            @block.tensor
            def _(pe):
                with out_of_range(pe):
                    pe.wait_ge(g_const, 2 + 2 * HG)
                    with pe.Fori(0, B) as b:
                        for g in range(G):
                            n = G * b + g
                            for dst, w in ((pz, wa_sb), (pk, wk_sb), (pq, wq_sb), (pv, wv_sb)):
                                mm = nc.tensor.matmul(dst[:, 0:T], w[:, g * P:(g + 1) * P], xnT[:, bass.ds(b * T, T)],
                                                      start=True, stop=True)
                            mm.then_inc(g_proj, 1)
                            pe.wait_ge(g_act, 4 * (n + 1))
                            nc.tensor.matmul(pn[:, 0:T], same_head[:], g_k2[:], start=True, stop=True).then_inc(g_ss, 1)
                            pe.wait_ge(g_in, n + 1)

                            def column(i, start, stop):
                                m = DH * n + i
                                pe.wait_ge(g_sel, 2 * (m + 1))
                                nc.tensor.matmul(pb[:, 0:T], spread[:].rearrange("p h d -> p (h d)"), g_v[:],
                                                 start=True, stop=True).then_inc(g_row, 1)
                                pe.wait_ge(g_qs_done, m + 1)
                                nc.tensor.matmul(po[:, 0:T], place[:], g_qs[:], start=start, stop=stop,
                                                 skip_group_check=True).then_inc(g_summed, 1)

                            column(0, True, False)
                            with pe.Fori(1, DH - 1) as i:
                                column(i, False, False)
                            column(DH - 1, False, True)
                            pe.wait_ge(g_out, n + 1)
                        for t in range(TPB):
                            for g in range(G):
                                mm = nc.tensor.matmul(py[:, t * D:(t + 1) * D], g_o[:, g, t * P:(t + 1) * P],
                                                      wo_sb[:, g, :], start=g == 0, stop=g == G - 1)
                        mm.then_inc(g_y, 1)
                        pe.wait_ge(g_y_done, b + 1)

            @block.scalar
            def _(act):
                with out_of_range(act):
                    with act.Fori(0, B) as b:
                        for g in range(G):
                            n = G * b + g
                            act.wait_ge(g_proj, n + 1)
                            act.wait_ge(g_z, n + 1)
                            nc.scalar.activation(g_a[:], g_a[:], ACT.Exp, scale=-1.0).then_inc(g_act, 1)
                            nc.scalar.activation(g_k2[:], pk[:, 0:T], ACT.Square).then_inc(g_act, 1)
                            nc.scalar.copy(g_q[:], pq[:, 0:T]).then_inc(g_act, 1)
                            nc.scalar.copy(g_v[:], pv[:, 0:T]).then_inc(g_act, 1)
                            act.wait_ge(g_clamped, n + 1)
                            nc.scalar.activation(g_n[:], g_n[:], ACT.Sqrt).then_inc(g_norm, 1)

            @block.vector
            def _(dve):
                with out_of_range(dve):
                    dve.wait_ge(g_const, 2 + 2 * HG)
                    with dve.Fori(0, B) as b:
                        for g in range(G):
                            n = G * b + g
                            dve.wait_ge(g_proj, n + 1)
                            nc.vector.tensor_scalar(g_a[:], pz[:, 0:T], ba_sb[:, g:g + 1], SIGMOID_FLOOR,
                                                    ALU.add, ALU.max).then_inc(g_z, 1)
                            dve.wait_ge(g_act, 4 * (n + 1))
                            nc.vector.tensor_scalar(g_a[:], g_a[:], 1.0, None, ALU.add).then_inc(g_norm, 1)
                            dve.wait_ge(g_ss, n + 1)
                            nc.vector.tensor_scalar(g_n[:], pn[:, 0:T], NORM_EPS ** 2, None, ALU.max).then_inc(g_clamped, 1)
                            dve.wait_ge(g_norm, 4 * n + 2)
                            nc.vector.reciprocal(g_a[:], g_a[:]).then_inc(g_norm, 1)
                            nc.vector.reciprocal(g_n[:], g_n[:]).then_inc(g_norm, 1)
                            dve.wait_ge(g_norm, 4 * (n + 1))
                            nc.vector.tensor_tensor(g_k[:], pk[:, 0:T], g_n[:], ALU.mult).then_inc(g_in, 1)
                            with dve.Fori(0, DH) as i:
                                m = DH * n + i
                                dve.wait_ge(g_in, n + 1)
                                unit = ident[:].rearrange("p (h d) -> p h d", h=HG)[:, :, bass.ds(i, 1)]
                                nc.vector.tensor_scalar(spread[:], unit.to_broadcast([P, HG, DH]), 1.0, None,
                                                        ALU.mult).then_inc(g_sel, 1)
                                nc.vector.tensor_scalar(place[:], window[:, bass.ds(DH - i, P)], 1.0, None,
                                                        ALU.mult).then_inc(g_sel, 1)
                                dve.wait_ge(g_row, m + 1)
                                nc.vector.tensor_tensor(g_kv[:], g_k[:], pb[:, 0:T], ALU.mult).then_inc(g_kv_done, 1)
                                dve.wait_ge(g_kv_done, m + 1)
                                nc.vector.tensor_tensor_scan(g_s[:], g_a[:], g_kv[:], 0.0, ALU.mult,
                                                             ALU.add).then_inc(g_s_done, 1)
                                dve.wait_ge(g_s_done, m + 1)
                                nc.vector.tensor_tensor(g_qs[:], g_s[:], g_q[:], ALU.mult).then_inc(g_qs_done, 1)
                                dve.wait_ge(g_summed, m + 1)
                            dve.wait_ge(g_summed, DH * (n + 1))
                            nc.vector.tensor_copy(g_o[:, g, :], po[:, 0:T]).then_inc(g_out, 1)
                        dve.wait_ge(g_y, b + 1)
                        nc.vector.scalar_tensor_tensor(y_sb[:, bass.ds(TPB * b, TPB), :], x_sb[:, bass.ds(TPB * b, TPB), :],
                                                       2.0, py[:, 0:TPB * D].rearrange("p (n d) -> p n d", n=TPB),
                                                       ALU.mult, ALU.add).then_inc(g_y_done, 1)

        stage = sb("stage", [P, TOPK, NTILES, ROW])
        with nc.Block() as block, ExitStack() as c4:
            def sb4(name, shape, dt=F32):
                return c4.enter_context(nc.sbuf_tensor(name, shape, dt))

            TG = 8
            NG = NTILES // TG
            st = sb4("st", [P, NTILES, 6])
            mean, var, tmp, rs = (sb4(n, [P, NTILES]) for n in ("mean", "var", "tmp", "rs"))
            slot_i = sb4("slot_i", [P, TOPK, NTILES], I32)
            x1T = sb4("x1T", [P, TG * P])
            probs, pr2, tie, rank, both = (sb4(n, [P, TG, E]) for n in ("probs", "pr2", "tie", "rank", "both"))
            chosen = sb4("chosen", [P, TOPK, TG, E])
            low, wsum, top = sb4("low", [P, TG]), sb4("wsum", [P, TG]), sb4("top", [P, TOPK, TG])
            slot_e, slot_f = sb4("slot_e", [P, TOPK, TG, E]), sb4("slot_f", [P, TOPK, TG])
            pT = [c4.enter_context(nc.psum_tensor(f"r_pT{i}", [P, 512], F32)) for i in range(2)]
            pL = [c4.enter_context(nc.psum_tensor(f"r_pL{i}", [P, 512], F32)) for i in range(2)]
            pR = c4.enter_context(nc.psum_tensor("r_pR", [P, 512], F32))
            before = pR[:, 0:TG * E].rearrange("p (t e) -> p t e", t=TG)
            total = pR[:, TG * E:(TG + 1) * E]
            HALF = TG // 2

            m_bn, m_join, m_rs, m_x1, m_x1b = sem("m_bn"), sem("m_join"), sem("m_rs"), sem("m_x1"), sem("m_x1b")
            m_xt, m_x1T, m_logits, m_exp, m_route = sem("m_xt"), sem("m_x1T"), sem("m_logits"), sem("m_exp"), sem("m_route")
            m_both, m_ranks, m_slots = sem("m_both"), sem("m_ranks"), sem("m_slots")
            ROUTE = 25

            def logits(n):
                return pL[n % 2][:, 0:TG * E].rearrange("p (t e) -> p t e", t=TG)

            @block.tensor
            def _(pe):
                def turn_x1(n):
                    for a in range(2):
                        pe.wait_ge(m_x1, TG * n + HALF * (a + 1))
                        at_least(pe, m_x1T, 2 * (n - 1) + a + 1)
                        for t in range(HALF):
                            mm = nc.tensor.transpose(pT[a][:, t * P:(t + 1) * P],
                                                     stage[:, 0, n * TG + a * HALF + t, 0:D], ident[:])
                        mm.then_inc(m_xt, 1)
                    pe.wait_ge(m_x1T, 2 * (n + 1))
                    for t in range(TG):
                        mm = nc.tensor.matmul(logits(n)[:, t, :], x1T[:, t * P:(t + 1) * P], wr_sb[:], start=True, stop=True)
                    mm.then_inc(m_logits, 1)

                pe.wait_ge(s_wr, 16)
                turn_x1(0)
                for n in range(NG):
                    if n + 1 < NG:
                        turn_x1(n + 1)
                    pe.wait_ge(m_both, n + 1)
                    nc.tensor.matmul(pR[:, 0:TG * E], earlier[:], both[:].rearrange("p t e -> p (t e)"),
                                     start=True, stop=False, skip_group_check=True)
                    for u in range(TG - 1):
                        nc.tensor.matmul(before[:, u + 1:TG, :], all_ones[:],
                                         both[:, u:u + 1, :].to_broadcast([P, TG - 1 - u, E]),
                                         start=False, stop=u == TG - 2, skip_group_check=True)
                    for u in range(TG):
                        mm = nc.tensor.matmul(total, all_ones[:], both[:, u, :], start=u == 0, stop=u == TG - 1)
                    mm.then_inc(m_ranks, 1)

            @block.scalar
            def _(act):
                load_table(EXP_LN_SET)

                def deviations_turned(n):
                    tl = slice(n * TG, (n + 1) * TG)
                    act.wait_ge(m_join, 6 * (n + 1))
                    nc.scalar.activation(rs[:, tl], var[:, tl], ACT.Ln, bias=eps_sb[:, 0:1]).then_inc(m_rs, 1)
                    act.wait_ge(m_rs, 2 * n + 1)
                    nc.scalar.activation(rs[:, tl], rs[:, tl], ACT.Exp, scale=-0.5).then_inc(m_rs, 1)
                    at_least(act, m_logits, n)
                    for a in range(2):
                        act.wait_ge(m_xt, 2 * n + a + 1)
                        nc.scalar.copy(x1T[:, a * HALF * P:(a + 1) * HALF * P], pT[a][:]).then_inc(m_x1T, 1)

                def second_rows(n):
                    tl = slice(n * TG, (n + 1) * TG)
                    nc.scalar.copy(stage[:, 1, tl, 0:D], stage[:, 0, tl, 0:D]).then_inc(m_x1b, 1)

                deviations_turned(0)
                second_rows(0)
                for n in range(NG):
                    if n + 1 < NG:
                        deviations_turned(n + 1)
                    act.wait_ge(m_route, ROUTE * n + 2)
                    nc.scalar.activation(probs[:], probs[:], ACT.Exp).then_inc(m_exp, 1)
                    if n + 1 < NG:
                        second_rows(n + 1)

            @block.sync
            def _(sp):
                sp.wait_ge(m_pad, 1)
                for e in range(E):
                    row = sp.value_load(pad_i[0:1, e:e + 1], min_val=0, max_val=NROWS - P)
                    sp.dma_start(rows_d[bass.ds(row, P), :], empty[:]).then_inc(s_pads, 16)
                sp.wait_ge(s_pads, 16 * E)

            @block.gpsimd
            def _(pool):
                pool.wait_ge(s_fill, 16)
                for n in range(NG):
                    pool.wait_ge(m_slots, n + 1)
                    pool.sem_inc(s_turn, 1)
                    for t in range(n * TG, (n + 1) * TG):
                        for k in range(TOPK):
                            nc.gpsimd.indirect_dma_start(
                                out=rows_d[:, :], out_offset=bass.IndirectOffsetOnAxis(ap=slot_i[:, k, t:t + 1], axis=0),
                                in_=stage[:, k, t, :], in_offset=None).then_inc(s_sent, 16)
                pool.wait_ge(s_sent, 16 * TOPK * NTILES)

            @block.vector
            def _(dve):
                def normalise(n):
                    tl = slice(n * TG, (n + 1) * TG)
                    for t in range(n * TG, (n + 1) * TG):
                        nc.vector.bn_stats(st[:, t, :], y_sb[:, t, :]).then_inc(m_bn, 1)
                    dve.wait_ge(m_bn, TG * (n + 1))
                    join_halves(dve, st[:, tl], mean[:, tl], var[:, tl], tmp[:, tl], m_join, 6 * n)
                    dve.wait_ge(m_rs, 2 * (n + 1))
                    for t in range(n * TG, (n + 1) * TG):
                        nc.vector.tensor_scalar(stage[:, 0, t, 0:D], y_sb[:, t, :], mean[:, t:t + 1], rs[:, t:t + 1],
                                                ALU.subtract, ALU.mult).then_inc(m_x1, 1)

                def route(n):
                    tl = slice(n * TG, (n + 1) * TG)
                    did = [0]

                    def then(ins):
                        did[0] += 1
                        ins.then_inc(m_route, 1)
                        dve.wait_ge(m_route, ROUTE * n + did[0])

                    def over(v):
                        return v.unsqueeze(2).to_broadcast([P, TG, E])

                    idx = iota8[:].unsqueeze(1).to_broadcast([P, TG, E])
                    dve.wait_ge(m_logits, n + 1)
                    then(nc.vector.tensor_reduce(low[:], logits(n), AXIS.X, ALU.max))
                    then(nc.vector.tensor_tensor(probs[:], logits(n), over(low[:]), ALU.subtract))
                    dve.wait_ge(m_exp, n + 1)
                    then(nc.vector.tensor_reduce(low[:], probs[:], AXIS.X, ALU.add))
                    then(nc.vector.reciprocal(low[:], low[:]))
                    then(nc.vector.tensor_tensor(probs[:], probs[:], over(low[:]), ALU.mult))
                    cur = probs
                    for k in range(TOPK):
                        then(nc.vector.tensor_reduce(top[:, k, :], cur[:], AXIS.X, ALU.max))
                        then(nc.vector.tensor_tensor(tie[:], cur[:], over(top[:, k, :]), ALU.is_equal))
                        then(nc.vector.tensor_tensor(tie[:], tie[:], idx, ALU.mult))
                        then(nc.vector.tensor_reduce(low[:], tie[:], AXIS.X, ALU.min))
                        then(nc.vector.tensor_tensor(chosen[:, k], idx, over(low[:]), ALU.is_equal))
                        if k == 0:
                            then(nc.vector.scalar_tensor_tensor(pr2[:], chosen[:, 0], -2.0, probs[:], ALU.mult, ALU.add))
                            cur = pr2
                    nc.vector.tensor_tensor(both[:], chosen[:, 0], chosen[:, 1], ALU.add).then_inc(m_both, 1)
                    then(nc.vector.tensor_tensor(wsum[:], top[:, 0, :], top[:, 1, :], ALU.add))
                    then(nc.vector.reciprocal(wsum[:], wsum[:]))
                    then(nc.vector.tensor_tensor(stage[:, :, tl, D], top[:], wsum[:].unsqueeze(1).to_broadcast([P, TOPK, TG]),
                                                 ALU.mult))
                    then(nc.vector.tensor_copy(stage[:, :, tl, D + 1], made_to[:, :, tl]))
                    dve.wait_ge(m_ranks, n + 1)
                    then(nc.vector.tensor_tensor(rank[:], before, next_row[:].unsqueeze(1).to_broadcast([P, TG, E]), ALU.add))
                    then(nc.vector.tensor_tensor(next_row[:], next_row[:], total, ALU.add))
                    for k in range(TOPK):
                        then(nc.vector.tensor_tensor(slot_e[:, k], chosen[:, k], rank[:], ALU.mult))
                    then(nc.vector.tensor_reduce(slot_f[:].rearrange("p k t -> p (k t)"),
                                                 slot_e[:].rearrange("p k t e -> p (k t) e"), AXIS.X, ALU.add))
                    assert did[0] == ROUTE, did
                    dve.wait_ge(m_x1b, n + 1)
                    nc.vector.tensor_copy(slot_i[:, :, tl], slot_f[:]).then_inc(m_slots, 1)

                dve.wait_ge(s_const, CONSTS)
                nc.vector.tensor_copy(next_row[:], first_row[:]).then_inc(m_first, 1)
                dve.wait_ge(m_first, 1)
                normalise(0)
                for n in range(NG):
                    if n + 1 < NG:
                        normalise(n + 1)
                    route(n)
                nc.vector.tensor_copy(pad_i[:], next_row[:]).then_inc(m_pad, 1)

                done = [0]

                def then(ins):
                    done[0] += 1
                    ins.then_inc(m_table, 1)
                    dve.wait_ge(m_table, done[0])

                then(nc.vector.tensor_tensor(count[:], next_row[:], first_row[:], ALU.subtract))
                then(nc.vector.tensor_tensor(full[:], count[:].unsqueeze(2).to_broadcast([P, E, NTILES]),
                                             tile_edge[:, 0:NTILES].unsqueeze(1).to_broadcast([P, E, NTILES]), ALU.is_gt))
                then(nc.vector.tensor_reduce(ntile[:], full[:], AXIS.X, ALU.add))
                then(nc.vector.tensor_tensor_scan(tiles_to[:], ones8[:], ntile[:], 0.0, ALU.mult, ALU.add))
                then(nc.vector.tensor_tensor(tiles_from[:], tiles_to[:], ntile[:], ALU.subtract))
                num = tile_no[:].unsqueeze(2).to_broadcast([P, NSLOT, E])

                def each(v):
                    return v.unsqueeze(1).to_broadcast([P, NSLOT, E])

                then(nc.vector.tensor_tensor(mine[:], num, each(tiles_from[:]), ALU.is_ge))
                then(nc.vector.tensor_tensor(work[:], num, each(tiles_to[:]), ALU.is_ge))
                then(nc.vector.tensor_tensor(mine[:], mine[:], work[:], ALU.subtract))
                then(nc.vector.tensor_tensor(work[:], mine[:], each(expert_no[:]), ALU.mult))
                then(nc.vector.tensor_reduce(slot_tab[:], work[:], AXIS.X, ALU.add))
                then(nc.vector.tensor_copy(expert_i[:], slot_tab[:]))
                then(nc.vector.tensor_tensor(work[:], num, each(tiles_from[:]), ALU.subtract))
                then(nc.vector.tensor_scalar(work[:], work[:], float(P), None, ALU.mult))
                then(nc.vector.tensor_tensor(work[:], work[:], each(first_row[:]), ALU.add))
                then(nc.vector.tensor_scalar(work[:], work[:], float(EMPTY_ROW), None, ALU.subtract))
                then(nc.vector.tensor_tensor(work[:], work[:], mine[:], ALU.mult))
                then(nc.vector.tensor_reduce(slot_tab[:], work[:], AXIS.X, ALU.add))
                then(nc.vector.tensor_scalar(slot_tab[:], slot_tab[:], float(EMPTY_ROW), None, ALU.add))
                then(nc.vector.tensor_copy(row_i[:], slot_tab[:]))

        with nc.Block() as block, ExitStack() as c5:
            def sb5(name, shape, dt=F32):
                return c5.enter_context(nc.sbuf_tensor(name, shape, dt))

            def ps5(name, shape):
                return c5.enter_context(nc.psum_tensor(name, shape, F32))

            xt = sb5("xt", [P, 4, ROW])
            xT = sb5("xT", [P, 2, P])
            sg = sb5("sg", [P, 2, F])
            hid = sb5("hid", [P, 2, F])
            hT = sb5("hT", [P, 2, FC, P])
            yt = sb5("yt", [P, 4, D])
            to_f = sb5("to_f", [P, 4])
            to_i = sb5("to_i", [P, 4], I32)
            pX = ps5("pX", [P, 512])
            pG = [ps5(f"pG{i}", [P, F]) for i in range(2)]
            pU = [ps5(f"pU{i}", [P, F]) for i in range(2)]
            pH = ps5("pH", [P, FC, P])
            pD = [ps5(f"pD{i}", [P, 512]) for i in range(2)]

            t_xt, t_xT, t_gate, t_up = sem("t_xt"), sem("t_xT"), sem("t_gate"), sem("t_up")
            t_load = [sem(f"t_load{i}") for i in range(4)]
            t_silu, t_hid, t_ht, t_hT, t_down, t_y = sem("t_silu"), sem("t_hid"), sem("t_ht"), sem("t_hT"), sem("t_down"), sem("t_y")
            t_to = sem("t_to")
            t_made = [sem(f"t_made{r}") for r in range(4)]

            def tiles(eng, step):
                for j in range(4):
                    step(j, j, 1)
                with eng.Fori(1, NSLOT // 4 - 1) as q:
                    for r in range(4):
                        step(4 * q + r, r, q + 1)
                for r in range(4):
                    step(NSLOT - 4 + r, r, NSLOT // 4)

            def ahead(j, r, turn, by):
                if isinstance(j, int) and j >= NSLOT - by:
                    return None
                return j + by, (r + by) % 4, turn + (r + by) // 4

            @block.sync
            def _(sp):
                sp.wait_ge(m_table, TABLE)

                def step(j, r, turn):
                    row = sp.value_load(row_i[0:1, bass.ds(j, 1)], min_val=0, max_val=NROWS - P)
                    at_least(sp, t_y, 3 * (j - 3))
                    sp.dma_start(xt[:, r, :], rows_d[bass.ds(row, P), :]).then_inc(t_load[r], 16)

                tiles(sp, step)

            @block.tensor
            def _(pe):
                pe.wait_ge(s_wm, 48)
                pe.wait_ge(m_table, TABLE)

                def weights(w, e):
                    return w[:, bass.ds(e, 1), :].rearrange("p a f -> p (a f)")

                def turn_rows(j, r, turn):
                    pe.wait_ge(t_load[r], 16 * turn)
                    at_least(pe, t_xT, j)
                    nc.tensor.transpose(pX[:, 0:P], xt[:, r, 0:D], ident[:]).then_inc(t_xt, 1)

                def expert(j):
                    return pe.value_load(expert_i[0:1, bass.ds(j, 1)], min_val=0, max_val=E - 1)

                def gate_up(j, r, e):
                    p = r % 2
                    pe.wait_ge(t_xT, j + 1)
                    at_least(pe, t_silu, j - 1)
                    nc.tensor.matmul(pG[p][:], xT[:, p, :], weights(w1_sb, e), start=True, stop=True).then_inc(t_gate, 1)
                    at_least(pe, t_hid, j - 1)
                    nc.tensor.matmul(pU[p][:], xT[:, p, :], weights(w3_sb, e), start=True, stop=True).then_inc(t_up, 1)

                def turn_hidden(j, r):
                    pe.wait_ge(t_hid, j + 1)
                    at_least(pe, t_hT, j)
                    for c in range(FC):
                        mm = nc.tensor.transpose(pH[:, c, :], hid[:, r % 2, c * P:(c + 1) * P], ident[:])
                    mm.then_inc(t_ht, 1)

                def down(j, r):
                    e = pe.value_load(expert_i[0:1, bass.ds(j, 1)], min_val=0, max_val=E - 1)
                    pe.wait_ge(t_hT, j + 1)
                    at_least(pe, t_y, 3 * (j - 1))
                    for c in range(FC):
                        mm = nc.tensor.matmul(pD[r % 2][:, 0:D], hT[:, r % 2, c, :],
                                              w2_sb[:, bass.ds(e, 1), c, :].rearrange("p a d -> p (a d)"),
                                              start=c == 0, stop=c == FC - 1)
                    mm.then_inc(t_down, 1)

                turn_rows(0, 0, 1)
                turn_rows(1, 1, 1)
                gate_up(0, 0, expert(0))

                def step(j, r, turn):
                    one, two = ahead(j, r, turn, 1), ahead(j, r, turn, 2)
                    if one:
                        e = expert(one[0])
                    turn_hidden(j, r)
                    if one:
                        gate_up(*one[:2], e)
                    if two:
                        turn_rows(*two)
                    down(j, r)

                tiles(pe, step)

            @block.scalar
            def _(act):
                def copy_x(j, r):
                    act.wait_ge(t_xt, j + 1)
                    at_least(act, t_up, j - 1)
                    nc.scalar.copy(xT[:, r % 2, :], pX[:, 0:P]).then_inc(t_xT, 1)

                def silu(j, r):
                    act.wait_ge(t_gate, j + 1)
                    at_least(act, t_hid, j - 1)
                    nc.scalar.activation(sg[:, r % 2, :], pG[r % 2][:], ACT.Silu).then_inc(t_silu, 1)

                copy_x(0, 0)
                copy_x(1, 1)
                silu(0, 0)

                def step(j, r, turn):
                    one, two = ahead(j, r, turn, 1), ahead(j, r, turn, 2)
                    act.wait_ge(t_ht, j + 1)
                    at_least(act, t_down, j - 1)
                    nc.scalar.copy(hT[:, r % 2], pH[:]).then_inc(t_hT, 1)
                    if one:
                        silu(*one[:2])
                    if two:
                        copy_x(*two[:2])

                tiles(act, step)

            @block.vector
            def _(dve):
                def hidden(j, r):
                    p = r % 2
                    dve.wait_ge(t_silu, j + 1)
                    dve.wait_ge(t_up, j + 1)
                    at_least(dve, t_ht, j - 1)
                    nc.vector.tensor_tensor(hid[:, p, :], pU[p][:], sg[:, p, :], ALU.mult).then_inc(t_hid, 1)

                hidden(0, 0)

                def step(j, r, turn):
                    one = ahead(j, r, turn, 1)
                    if one:
                        hidden(*one[:2])
                    dve.wait_ge(t_load[r], 16 * turn)
                    at_least(dve, t_made[r], 16 * (turn - 1))
                    nc.vector.tensor_scalar(to_f[:, r:r + 1], xt[:, r, D + 1:D + 2], float(TOPK * NT), tile_edge[:, bass.ds(j, 1)],
                                            ALU.is_ge, ALU.mult).then_inc(t_to, 1)
                    dve.wait_ge(t_to, j + 1)
                    nc.vector.tensor_tensor(to_i[:, r:r + 1], to_f[:, r:r + 1], xt[:, r, D + 1:D + 2],
                                            ALU.add).then_inc(t_y, 1)
                    dve.wait_ge(t_down, j + 1)
                    nc.vector.tensor_scalar(yt[:, r, :], pD[r % 2][:, 0:D], xt[:, r, D:D + 1], None, ALU.mult).then_inc(t_y, 2)

                tiles(dve, step)

            @block.gpsimd
            def _(pool):
                def step(j, r, turn):
                    p = r % 2
                    pool.wait_ge(t_y, 3 * (j + 1))
                    pool.sem_inc(s_turn, 1)
                    nc.gpsimd.indirect_dma_start(
                        out=made_d[:, :], out_offset=bass.IndirectOffsetOnAxis(ap=to_i[:, r:r + 1], axis=0),
                        in_=yt[:, r, :], in_offset=None).then_inc(t_made[r], 16)

                tiles(pool, step)
                for r in range(4):
                    pool.wait_ge(t_made[r], 16 * (NSLOT // 4))

        with nc.Block() as block, ExitStack() as c6:
            def sb6(name, shape, dt=F32):
                return c6.enter_context(nc.sbuf_tensor(name, shape, dt))

            made = sb6("made", [P, TOPK, NTILES, D])
            fx = sb6("fx", [P, 2, TB, D])
            fo = sb6("fo2", [P, 4, TB, D])
            fst = sb6("fst2", [P, TB, 6])
            fmean, fvar, ftmp, frs = (sb6(n + "2", [P, TB]) for n in ("fmean", "fvar", "ftmp", "frs"))
            f_load = [sem(f"f_load{n}") for n in range(NBLK)]
            f_bn, f_join, f_rs, f_fo = sem("f_bn"), sem("f_join"), sem("f_rs"), sem("f_fo")
            f_sum = sem("f_sum")
            f_out = [sem(f"f_out{k}") for k in range(4)]

            @block.sync
            def _(sp):
                made_v = made_d[0:TOPK * NT, :].rearrange("(k n p) d -> p k n d", p=P, k=TOPK)
                for n in range(NBLK):
                    for k in range(TOPK):
                        sp.dma_start(made[:, k, n * TB:(n + 1) * TB, :],
                                     made_v[:, k, n * TB:(n + 1) * TB, :]).then_inc(f_load[n], 16)
                for n in range(NBLK):
                    sp.wait_ge(f_fo, TB * (n + 1))
                    sp.dma_start(out_d[:, n * TB:(n + 1) * TB, :], fo[:, n % 4]).then_inc(f_out[n % 4], 16)
                for k in range(4):
                    sp.wait_ge(f_out[k], 16 * (NBLK // 4))

            @block.scalar
            def _(act):
                load_table(EXP_LN_SET)
                for n in range(NBLK):
                    act.wait_ge(f_join, 6 * (n + 1))
                    nc.scalar.activation(frs[:], fvar[:], ACT.Ln, bias=eps_sb[:, 0:1]).then_inc(f_rs, 1)
                    act.wait_ge(f_rs, 2 * n + 1)
                    nc.scalar.activation(frs[:], frs[:], ACT.Exp, scale=-0.5).then_inc(f_rs, 1)

            @block.vector
            def _(dve):
                for n in range(NBLK):
                    dve.wait_ge(f_load[n], 16 * TOPK)
                    f = fx[:, n % 2]
                    blk = slice(n * TB, (n + 1) * TB)
                    nc.vector.tensor_tensor(f, made[:, 0, blk, :], made[:, 1, blk, :], ALU.add).then_inc(f_sum, 1)
                    dve.wait_ge(f_sum, 2 * n + 1)
                    nc.vector.tensor_tensor(f, f, stage[:, 0, blk, 0:D], ALU.add).then_inc(f_sum, 1)
                    dve.wait_ge(f_sum, 2 * n + 2)
                    for t in range(TB):
                        nc.vector.bn_stats(fst[:, t, :], f[:, t, :]).then_inc(f_bn, 1)
                    dve.wait_ge(f_bn, TB * (n + 1))
                    join_halves(dve, fst, fmean, fvar, ftmp, f_join, 6 * n)
                    dve.wait_ge(f_rs, 2 * (n + 1))
                    at_least(dve, f_out[n % 4], 16 * (n // 4))
                    for t in range(TB):
                        nc.vector.tensor_scalar(fo[:, n % 4, t, :], f[:, t, :], fmean[:, t:t + 1], frs[:, t:t + 1],
                                                ALU.subtract, ALU.mult).then_inc(f_fo, 1)


_INS = ["L0_attn_x", "L0_attn_Wq", "L0_attn_Wk", "L0_attn_Wv", "L0_attn_Wa", "L0_attn_ba", "L0_attn_Wo",
        "L0_attn_gamma", "L0_attn_beta", "L0_ffn_Wr", "L0_ffn_W1", "L0_ffn_W2", "L0_ffn_W3"]


def kernel(**inputs):
    import numpy as np
    import concourse.bacc as bacc
    from concourse import mybir as mb
    from concourse.bass_utils import run_bass_kernel_spmd

    nc = bacc.Bacc("TRN2", target_bir_lowering=False, num_devices=1)
    arrays, args = {}, []
    for name in _INS:
        a = np.asarray(inputs[name])
        if name == "L0_ffn_Wr":
            a = a.T
        if name == "L0_attn_ba":
            a = a.reshape(-1, 128).T
        a = np.ascontiguousarray(a)
        arrays[f"in_{name}"] = a
        args.append(nc.dram_tensor(f"in_{name}", a.shape, mb.dt.from_np(a.dtype), kind="ExternalInput").ap())
    shape = tuple(inputs["L0_attn_x"].shape)
    out = nc.dram_tensor("out_0", shape, mb.dt.float32, kind="ExternalOutput").ap()
    build(nc, *args, out)
    r = run_bass_kernel_spmd(nc, [arrays], core_ids=[0])
    return r.results[0]["out_0"]
```

```python
import math
from contextlib import ExitStack

import concourse.bass as bass
import concourse.mybir as mybir

P = 128
F32 = mybir.dt.float32
I32 = mybir.dt.int32
F32R = mybir.dt.float32r
ALU = mybir.AluOpType
ACT = mybir.ActivationFunctionType
AXIS = mybir.AxisListType

LN_EPS = 1e-5
NORM_EPS = 1e-12
DECAY_LIMIT = 40.0
SS_SCALE = 2.0 ** 20
GATE_FLOOR = -40.0
SIGMOID_FLOOR = -87.0


def at_least(eng, sem, count):
    if isinstance(count, int) and count <= 0:
        return
    eng.wait_ge(sem, count)


def build(nc, x, wq, wk, wv, wa, ba_t, wo, gamma, beta, wr_t, w1, w2, w3, out):
    B, T, D = x.shape
    DI = wq.shape[1]
    G = DI // P
    HG = 2
    H = G * HG
    DH = DI // H
    E, _, F = w1.shape
    FC = F // P
    NT = B * T
    TPB = T // P
    NTILES = NT // P
    BLK = 512
    TB = BLK // P
    NBLK = NT // BLK
    GT = G * T

    TOPK = 2
    ROW = D + 2
    PART = NT + P
    EMPTY_ROW = E * PART
    NROWS = EMPTY_ROW + P
    NSLOT = TOPK * NTILES + E
    CONSTS = 14
    TABLE = 19
    EXP_LN_SET = 6

    rows_d = nc.dram_tensor("expert_rows", [NROWS, ROW], F32).ap()
    made_d = nc.dram_tensor("made_rows", [TOPK * NT + NSLOT * P, D], F32).ap()
    x_d = x.rearrange("b t d -> (b t) d").rearrange("(n p) d -> p n d", p=P)
    out_d = out.rearrange("b t d -> (b t) d").rearrange("(n p) d -> p n d", p=P)

    with ExitStack() as ctx:
        def sb(name, shape, dt=F32):
            return ctx.enter_context(nc.sbuf_tensor(name, shape, dt))

        def sem(name):
            return ctx.enter_context(nc.semaphore(name))

        y_sb = sb("y_sb", [P, NTILES, D])
        w2_sb = sb("w2_sb", [P, E, FC, D])
        w1_lo = sb("w1_lo", [P, E, F], F32R)
        w3_lo = sb("w3_lo", [P, E, F], F32R)
        wr_sb = sb("wr_sb", [P, E])
        gamma_sb = sb("gamma_sb", [P, 1])
        beta_sb = sb("beta_sb", [P, 1])
        ident = sb("ident", [P, P])
        causal = sb("causal", [P, 3 * P])
        head_sel = sb("head_sel", [P, G, H])
        eps_sb = sb("eps_sb", [P, 1])
        log_scale = sb("log_scale", [P, 1])
        ones_col = sb("ones_col", [P, 1])
        iota8 = sb("iota8", [P, E])
        iota_i = sb("iota_i", [P, E], I32)
        earlier = sb("earlier", [P, P])
        all_ones = sb("all_ones", [P, P])
        first_row = sb("first_row", [P, E])
        next_row = sb("next_row", [P, E])
        made_i = sb("made_i", [P, TOPK * NTILES + 1], I32)
        made_to = sb("made_to", [P, TOPK, NTILES])
        lane_f = sb("lane_f", [P, 1])
        expert_no = sb("expert_no", [P, E])
        ones8 = sb("ones8", [P, E])
        tile_no = sb("tile_no", [P, NSLOT])
        tile_edge = sb("tile_edge", [P, NSLOT])
        table_i = sb("table_i", [P, NSLOT], I32)
        lane_i = sb("lane_i", [P, 1], I32)
        empty = sb("empty", [P, ROW])
        pad_i = sb("pad_i", [P, E], I32)
        count, ntile, tiles_to, tiles_from = (sb(n, [P, E]) for n in ("count", "ntile", "tiles_to", "tiles_from"))
        full = sb("full", [P, E, NTILES])
        mine, work = sb("mine", [P, NSLOT, E]), sb("work", [P, NSLOT, E])
        slot_tab = sb("slot_tab", [P, NSLOT])
        expert_i, row_i = sb("expert_i", [P, NSLOT], I32), sb("row_i", [P, NSLOT], I32)
        rng_sb = sb("rng_sb", [P, B, G, 2])
        flag_f = sb("flag_f", [P, 1])
        flag_i = sb("flag_i", [P, 1], I32)

        att = ctx.enter_context(ExitStack())

        def sb_att(name, shape, dt=F32):
            return att.enter_context(nc.sbuf_tensor(name, shape, dt))

        x_sb = sb_att("x_sb", [P, NTILES, D])
        xnT = sb_att("xnT", [P, NT])
        wq_sb = sb_att("wq_sb", [P, DI])
        wk_sb = sb_att("wk_sb", [P, DI])
        wv_sb = sb_att("wv_sb", [P, DI])
        wa_sb = sb_att("wa_sb", [P, DI])
        wo_sb = sb_att("wo_sb", [P, G, D])
        ba_sb = sb_att("ba_sb", [P, G])
        keep = sb_att("keep", [P, G, T])

        s_x = [sem(f"x_loaded{n}") for n in range(4)]
        s_affine = sem("gamma_beta_bias_loaded")
        s_wa, s_wq, s_wk, s_wv, s_wo, s_wr = (sem(n + "_loaded") for n in ("wa", "wq", "wk", "wv", "wo", "wr"))
        s_wm = sem("expert_weights_loaded")
        s_id0 = sem("ident_zeroed")
        s_id = sem("ident_ready")
        s_const0 = sem("constants_filled")
        s_const = sem("constants_ready")
        s_iota = sem("iota_written")
        s_fill, s_pads, s_turn = sem("empty_rows_filled"), sem("empty_tiles_sent"), sem("pool_turn")
        s_sent = sem("rows_sent")
        m_first, m_pad, m_table = sem("m_first"), sem("m_pad"), sem("m_table")
        s_bn = sem("ln0_stats")
        s_ag = sem("ln0_aggregated")
        s_rs = sem("ln0_rstd")
        s_xh = sem("ln0_normalised")
        s_xt = sem("ln0_transposed")
        s_xn = sem("xnT_written")
        z_ready, q_ready, k_ready = sem("z_ready"), sem("q_ready"), sem("k_ready")
        v_ready, ss_ready = sem("v_ready"), sem("ss_ready")
        at_ready, av_done, o_ready, y_ready = sem("at_ready"), sem("av_done"), sem("o_ready"), sem("y_ready")
        z_done = sem("z_done")
        e_done, sp_done, sq_done = sem("e_done"), sem("sp_done"), sem("sq_done")
        eq_done, ek_done, o_copied = sem("eq_done"), sem("ek_done"), sem("o_copied")
        l_done, qd_done, kd_done = sem("l_done"), sem("qd_done"), sem("kd_done")
        masked, rn_done, vs_done = sem("masked"), sem("rn_done"), sem("vs_done")
        ss_done = sem("ss_done")
        y_done, rng_done = sem("y_done"), sem("rng_done")
        xs_done, lc_raw, lc_done = sem("xs_done"), sem("lc_raw"), sem("lc_done")
        s_fl = sem("flag_steps")
        s_flag_sum = sem("flag_sum")
        s_flag = sem("flag_ready")

        def load_table(number):
            nc.scalar.add_instruction(mybir.InstLoadActFuncSet(
                act_func_set_id=number, name=nc.get_next_instruction_name(),
                engine=mybir.EngineType.Activation, ins=[], outs=[]))

        def join_halves(dve, st, mean, var, tmp, done, base):
            nc.vector.tensor_tensor(mean[:], st[:, :, 1], st[:, :, 4], ALU.add).then_inc(done, 1)
            nc.vector.tensor_tensor(tmp[:], st[:, :, 1], st[:, :, 4], ALU.subtract).then_inc(done, 1)
            nc.vector.tensor_tensor(var[:], st[:, :, 2], st[:, :, 5], ALU.add).then_inc(done, 1)
            dve.wait_ge(done, base + 3)
            nc.vector.tensor_scalar(mean[:], mean[:], 0.5, None, ALU.mult).then_inc(done, 1)
            nc.vector.scalar_tensor_tensor(tmp[:], tmp[:], 0.25, tmp[:], ALU.mult, ALU.mult).then_inc(done, 1)
            dve.wait_ge(done, base + 5)
            nc.vector.scalar_tensor_tensor(var[:], var[:], 1.0 / D, tmp[:], ALU.mult, ALU.add).then_inc(done, 1)

        with nc.Block() as block, ExitStack() as c1:
            def sb1(name, shape):
                return c1.enter_context(nc.sbuf_tensor(name, shape, F32))

            def ps1(name, shape):
                return c1.enter_context(nc.psum_tensor(name, shape, F32))

            xs = sb1("xs", [P, 2, T])
            sp = sb1("sp", [P, G, T])
            lsum = sb1("lsum", [P, G, T])
            lc = sb1("lc", [P, G, T])
            eq = sb1("eq", [P, G, T])
            ek = sb1("ek", [P, G, T])
            k2 = sb1("k2", [P, G, T])
            qd = sb1("qd", [P, 2, G, T])
            kd = sb1("kd", [P, 2, G, T])
            vs = sb1("vs", [P, 2, TPB, DI])
            ss = sb1("ss", [P, TPB, H])
            rn = sb1("rn", [P, TPB, H])
            am = sb1("am", [P, 4, 3 * P])
            ob = sb1("ob", [P, G, T])
            NX = 4
            XT, BPX = NTILES // NX, NBLK // NX
            st0 = sb1("st0", [P, NTILES, 6])
            mean0, var0, rs0, tmp0 = (sb1(n, [P, NTILES]) for n in ("mean0", "var0", "rs0", "tmp0"))
            pA = ps1("pA", [P, G, T])
            pB = ps1("pB", [P, G * T])
            pAT = [ps1(f"pAT{i}", [P, 512]) for i in range(2)]
            pO = [ps1(f"pO{i}", [P, HG, T]) for i in range(2)]
            turned = [pO[a][:].rearrange("p h t -> p (h t)") for a in range(BPX)]
            pV = pB[:, :].rearrange("p (n c) -> p n c", n=TPB)
            pQ = pB[:, :].rearrange("p (g t) -> p g t", g=G)
            pSS = pAT[1][:, 0:TPB * H].rearrange("p (n h) -> p n h", n=TPB)
            pY = pAT[0][:, 0:TPB * D].rearrange("p (n d) -> p n d", n=TPB)

            def rows(loop_engine, step):
                step(0, 0)
                step(1, 1)
                with loop_engine.Fori(1, B // 2 - 1) as j:
                    step(2 * j, 0)
                    step(2 * j + 1, 1)
                step(B - 2, 0)
                step(B - 1, 1)

            def of_part(n):
                return slice(n * XT, (n + 1) * XT)

            def is_last(i):
                return isinstance(i, int) and i == B - 1

            @block.sync
            def _(sync):
                for n in range(NX):
                    sync.dma_start(x_sb[:, of_part(n), :], x_d[:, of_part(n), :]).then_inc(s_x[n], 16)
                sync.dma_start(wv_sb[:], wv).then_inc(s_wv, 16)
                sync.dma_start(wo_sb[:], wo.rearrange("(g p) d -> p g d", p=P)).then_inc(s_wo, 16)
                sync.dma_start(wr_sb[:], wr_t).then_inc(s_wr, 16)
                sync.dma_start(w1_lo[:].bitcast(F32), w1.rearrange("e h f -> h e f")).then_inc(s_wm, 16)
                sync.dma_start(w2_sb[:], w2.rearrange("e (c p) h -> p e c h", p=P)).then_inc(s_wm, 16)

            @block.tensor
            def _(pe):
                def turn_x(n):
                    for a in range(BPX):
                        blk = n * BPX + a
                        pe.wait_ge(s_xh, TB * (blk + 1))
                        at_least(pe, s_xn, blk - BPX + 1)
                        for t in range(TB):
                            mm = nc.tensor.transpose(turned[a][:, t * P:(t + 1) * P], y_sb[:, blk * TB + t, :], ident[:])
                        mm.then_inc(s_xt, 1)

                def project(dst, w, b):
                    for g in range(G):
                        mm = nc.tensor.matmul(dst[:, g, :], w[:, g * P:(g + 1) * P], xnT[:, bass.ds(b * T, T)],
                                              start=True, stop=True)
                    return mm

                def gates(b):
                    at_least(pe, kd_done, b)
                    project(pA, wa_sb, b).then_inc(z_ready, 1)

                def queries(b):
                    at_least(pe, vs_done, b)
                    project(pQ, wq_sb, b).then_inc(q_ready, 1)

                def keys(b):
                    pe.wait_ge(z_done, G * (b + 1))
                    project(pA, wk_sb, b).then_inc(k_ready, 1)

                def v_norms(b, p):
                    pe.wait_ge(qd_done, b + 1)
                    pe.wait_ge(xs_done, b + 1)
                    for n in range(TPB):
                        mm = nc.tensor.matmul(pV[:, n, :], xs[:, p, n * P:(n + 1) * P], wv_sb[:],
                                              start=True, stop=True)
                    mm.then_inc(v_ready, 1)
                    pe.wait_ge(sq_done, b + 1)
                    at_least(pe, masked, H * b)
                    for n in range(TPB):
                        for g in range(G):
                            mm = nc.tensor.matmul(pSS[:, n, :], k2[:, g, n * P:(n + 1) * P], head_sel[:, g, :],
                                                  start=g == 0, stop=g == G - 1)
                    mm.then_inc(ss_ready, 1)

                def scores(b, p, h):
                    if h == 0:
                        pe.wait_ge(kd_done, b + 1)
                        pe.wait_ge(qd_done, b + 1)
                        at_least(pe, y_done, b)
                    elif h == 1:
                        pe.wait_ge(ss_done, b + 1)
                    else:
                        pe.wait_ge(masked, H * b + h - 1)
                    g, r = h // HG, slice(DH * (h % HG), DH * (h % HG) + DH)
                    at = pAT[h % 2]
                    nc.tensor.matmul(at[:, 0:T], kd[r, p, g, 0:P], qd[r, p, g, :], start=True, stop=True)
                    nc.tensor.matmul(at[:, T:T + P], kd[r, p, g, P:T], qd[r, p, g, P:T],
                                     start=True, stop=True).then_inc(at_ready, 1)

                def values(b, p, h):
                    if h == 0:
                        pe.wait_ge(vs_done, b + 1)
                        at_least(pe, o_copied, 2 * b - 1)
                    if h == H // 2:
                        at_least(pe, o_copied, 2 * b)
                    pe.wait_ge(masked, H * b + h + 1)
                    g, r = h // HG, slice(DH * (h % HG), DH * (h % HG) + DH)
                    o = pO[g // 2][r, g % 2, :]
                    nc.tensor.matmul(o, vs[:, p, 0, h * DH:(h + 1) * DH], am[:, h % 4, 0:T],
                                     start=True, stop=False, skip_group_check=True)
                    mm = nc.tensor.matmul(o[:, P:T], vs[:, p, 1, h * DH:(h + 1) * DH], am[:, h % 4, T:T + P],
                                          start=False, stop=True, skip_group_check=True)
                    mm.then_inc(av_done, 1)

                def project_out(b):
                    pe.wait_ge(o_copied, 2 * b + 2)
                    pe.wait_ge(masked, H * b + H - 1)
                    for n in range(TPB):
                        for g in range(G):
                            mm = nc.tensor.matmul(pY[:, n, :], ob[:, g, n * P:(n + 1) * P], wo_sb[:, g, :],
                                                  start=g == 0, stop=g == G - 1)
                    mm.then_inc(y_ready, 1)

                pe.wait_ge(s_id, 1)
                turn_x(0)
                pe.wait_ge(s_wa, 16)
                pe.wait_ge(s_xn, BPX)
                gates(0)
                turn_x(1)
                pe.wait_ge(s_wq, 16)
                queries(0)
                pe.wait_ge(s_wk, 16)
                keys(0)
                turn_x(2)
                pe.wait_ge(s_const, CONSTS)
                pe.wait_ge(s_wv, 16)
                v_norms(0, 0)
                turn_x(3)
                pe.wait_ge(s_xn, NBLK)
                pe.wait_ge(s_wo, 16)

                def step(i, p):
                    if not is_last(i):
                        gates(i + 1)
                    scores(i, p, 0)
                    scores(i, p, 1)
                    if not is_last(i):
                        queries(i + 1)
                    for h in range(H):
                        values(i, p, h)
                        if h + 2 < H:
                            scores(i, p, h + 2)
                        if h == 0 and not is_last(i):
                            keys(i + 1)
                    if not is_last(i):
                        v_norms(i + 1, 1 - p)
                    project_out(i)

                rows(pe, step)

            @block.scalar
            def _(act):
                act.dma_start(wa_sb[:], wa).then_inc(s_wa, 16)
                act.dma_start(gamma_sb[:], gamma.rearrange("(p a) -> p a", a=1)).then_inc(s_affine, 16)
                act.dma_start(beta_sb[:], beta.rearrange("(p a) -> p a", a=1)).then_inc(s_affine, 16)
                act.dma_start(ba_sb[:], ba_t).then_inc(s_affine, 16)
                act.dma_start(wq_sb[:], wq).then_inc(s_wq, 16)
                act.dma_start(wk_sb[:], wk).then_inc(s_wk, 16)
                act.dma_start(w3_lo[:].bitcast(F32), w3.rearrange("e h f -> h e f")).then_inc(s_wm, 16)
                load_table(EXP_LN_SET)

                def deviations(n):
                    tl = of_part(n)
                    act.wait_ge(s_ag, 6 * (n + 1))
                    nc.scalar.activation(rs0[:, tl], var0[:, tl], ACT.Ln, bias=eps_sb[:, 0:1]).then_inc(s_rs, 1)
                    act.wait_ge(s_rs, 2 * n + 1)
                    nc.scalar.activation(rs0[:, tl], rs0[:, tl], ACT.Exp, scale=-0.5).then_inc(s_rs, 1)

                def write_xn(n):
                    for a in range(BPX):
                        blk = n * BPX + a
                        act.wait_ge(s_xt, blk + 1)
                        nc.scalar.activation(xnT[:, blk * BLK:(blk + 1) * BLK], turned[a], ACT.Identity,
                                             scale=gamma_sb[:, 0:1], bias=beta_sb[:, 0:1]).then_inc(s_xn, 1)

                def gates(b):
                    act.wait_ge(z_done, G * (b + 1))
                    nc.scalar.activation(sp[:], sp[:], ACT.Exp, scale=-1.0).then_inc(e_done, 1)
                    act.wait_ge(e_done, b + 1)
                    nc.scalar.activation(sp[:], sp[:], ACT.Ln, bias=1.0).then_inc(sp_done, 1)

                def squares(b):
                    act.wait_ge(k_ready, b + 1)
                    at_least(act, ss_ready, b)
                    nc.scalar.activation(k2[:], pA[:], ACT.Square).then_inc(sq_done, 1)

                def decays(b):
                    act.wait_ge(lc_done, b + 1)
                    at_least(act, qd_done, b)
                    nc.scalar.activation(eq[:], lc[:], ACT.Exp, scale=-1.0).then_inc(eq_done, 1)
                    at_least(act, kd_done, b)
                    nc.scalar.activation(ek[:], lc[:], ACT.Exp).then_inc(ek_done, 1)

                def norms(b):
                    act.wait_ge(ss_done, b + 1)
                    at_least(act, vs_done, b)
                    nc.scalar.activation(rn[:], ss[:], ACT.Ln, scale=SS_SCALE).then_inc(rn_done, 1)
                    act.wait_ge(rn_done, 2 * b + 1)
                    nc.scalar.activation(rn[:], rn[:], ACT.Exp, scale=-0.5, bias=log_scale[:, 0:1]).then_inc(rn_done, 1)

                def copy_out(b, j):
                    act.wait_ge(av_done, H * b + 4 * (j + 1))
                    if j == 0:
                        at_least(act, y_ready, b)
                    nc.scalar.copy(ob[:, 2 * j:2 * j + 2, :], pO[j][:]).then_inc(o_copied, 1)

                act.wait_ge(s_id0, 2)
                deviations(0)
                deviations(1)
                act.wait_ge(s_affine, 16 * 3)
                write_xn(0)
                deviations(2)
                write_xn(1)
                gates(0)
                squares(0)
                deviations(3)
                write_xn(2)
                decays(0)
                write_xn(3)
                act.wait_ge(s_const, CONSTS)
                norms(0)

                def step(i, p):
                    if not is_last(i):
                        gates(i + 1)
                        squares(i + 1)
                        decays(i + 1)
                    copy_out(i, 0)
                    copy_out(i, 1)
                    if not is_last(i):
                        norms(i + 1)

                rows(act, step)

            @block.gpsimd
            def _(pool):
                nc.gpsimd.memset(ident[:], 0.0).then_inc(s_id0, 1)
                nc.gpsimd.memset(eps_sb[:], LN_EPS).then_inc(s_id0, 1)
                pool.wait_ge(s_id0, 2)
                nc.gpsimd.affine_select(out=ident[:], in_=ident[:], compare_op=ALU.not_equal, fill=1.0,
                                        base=0, pattern=[[-1, P]], channel_multiplier=1).then_inc(s_id, 1)
                nc.gpsimd.memset(causal[:], 1.0).then_inc(s_const0, 1)
                nc.gpsimd.memset(head_sel[:], 1.0).then_inc(s_const0, 1)
                nc.gpsimd.memset(ones_col[:], 1.0).then_inc(s_const0, 1)
                nc.gpsimd.memset(keep[:], 1.0).then_inc(s_const0, 1)
                nc.gpsimd.memset(log_scale[:], 0.5 * math.log(SS_SCALE)).then_inc(s_const0, 1)
                nc.gpsimd.iota(iota_i[:], pattern=[[1, E]], base=-E, channel_multiplier=0).then_inc(s_iota, 1)
                nc.gpsimd.memset(earlier[:], 1.0).then_inc(s_const0, 1)
                nc.gpsimd.memset(all_ones[:], 1.0).then_inc(s_const0, 1)
                nc.gpsimd.memset(ones8[:], 1.0).then_inc(s_const0, 1)
                nc.gpsimd.memset(empty[:], 0.0).then_inc(s_const0, 1)
                nc.gpsimd.iota(made_i[:], pattern=[[P, TOPK * NTILES + 1]], base=0, channel_multiplier=1).then_inc(s_iota, 1)
                nc.gpsimd.iota(table_i[:], pattern=[[1, NSLOT]], base=0, channel_multiplier=0).then_inc(s_iota, 1)
                nc.gpsimd.iota(lane_i[:], pattern=[[0, 1]], base=0, channel_multiplier=1).then_inc(s_iota, 1)
                pool.wait_ge(s_const0, 9)
                for c in (0, 2):
                    tri = causal[:, c * P:(c + 1) * P]
                    nc.gpsimd.affine_select(out=tri, in_=tri, compare_op=ALU.is_ge, fill=0.0,
                                            base=0, pattern=[[1, P]], channel_multiplier=-1).then_inc(s_const, 1)
                nc.gpsimd.affine_select(out=head_sel[:], in_=head_sel[:], compare_op=ALU.is_ge, fill=0.0,
                                        base=0, pattern=[[P, G], [-DH, H]],
                                        channel_multiplier=1).then_inc(s_const, 1)
                pool.wait_ge(s_const, 3)
                nc.gpsimd.affine_select(out=head_sel[:], in_=head_sel[:], compare_op=ALU.is_ge, fill=0.0,
                                        base=DH - 1, pattern=[[-P, G], [DH, H]],
                                        channel_multiplier=-1).then_inc(s_const, 1)
                nc.gpsimd.memset(keep[:, :, 0:1], 0.0).then_inc(s_const, 1)
                nc.gpsimd.affine_select(out=earlier[:], in_=earlier[:], compare_op=ALU.is_ge, fill=0.0,
                                        base=-1, pattern=[[1, P]], channel_multiplier=-1).then_inc(s_const, 1)
                pool.wait_ge(s_iota, 4)
                nc.gpsimd.tensor_copy(iota8[:], iota_i[:]).then_inc(s_const, 1)
                nc.gpsimd.tensor_copy(tile_no[:], table_i[:]).then_inc(s_const, 1)
                nc.gpsimd.tensor_copy(lane_f[:], lane_i[:]).then_inc(s_const, 1)
                nc.gpsimd.tensor_copy(empty[:, D + 1:D + 2], made_i[:, TOPK * NTILES:TOPK * NTILES + 1]).then_inc(s_const, 1)
                nc.gpsimd.tensor_copy(made_to[:].rearrange("p k n -> p (k n)"), made_i[:, 0:TOPK * NTILES]).then_inc(s_const, 1)
                pool.wait_ge(s_const, 11)
                nc.gpsimd.tensor_scalar(expert_no[:], iota8[:], float(E), None, ALU.add).then_inc(s_const, 1)
                nc.gpsimd.tensor_scalar(tile_edge[:], tile_no[:], float(P), None, ALU.mult).then_inc(s_const, 1)
                pool.wait_ge(s_const, 13)
                nc.gpsimd.tensor_scalar(first_row[:], expert_no[:], float(PART), None, ALU.mult).then_inc(s_const, 1)
                pool.wait_ge(s_const, 14)
                nc.gpsimd.dma_start(rows_d[EMPTY_ROW:NROWS, :], empty[:]).then_inc(s_fill, 16)

                def prepare(b, p):
                    if isinstance(b, int) and b < 2:
                        pool.wait_ge(s_xn, BPX if b == 0 else NBLK)
                    at_least(pool, v_ready, b - 1)
                    nc.gpsimd.tensor_copy(xs[:, p, :], xnT[:, bass.ds(b * T, T)]).then_inc(xs_done, 1)

                rows(pool, prepare)

            @block.vector
            def _(dve):
                flat = "p g t -> p (g t)"

                def statistics(n):
                    tl = of_part(n)
                    dve.wait_ge(s_x[n], 16)
                    for t in range(n * XT, (n + 1) * XT):
                        nc.vector.bn_stats(st0[:, t, :], x_sb[:, t, :]).then_inc(s_bn, 1)
                    dve.wait_ge(s_bn, XT * (n + 1))
                    join_halves(dve, st0[:, tl], mean0[:, tl], var0[:, tl], tmp0[:, tl], s_ag, 6 * n)

                def normalise(n):
                    dve.wait_ge(s_rs, 2 * (n + 1))
                    for t in range(n * XT, (n + 1) * XT):
                        nc.vector.tensor_scalar(y_sb[:, t, :], x_sb[:, t, :], mean0[:, t:t + 1], rs0[:, t:t + 1],
                                                ALU.subtract, ALU.mult).then_inc(s_xh, 1)

                def gate_logits(b, p):
                    dve.wait_ge(z_ready, b + 1)
                    at_least(dve, l_done, b)
                    for g in range(G):
                        nc.vector.tensor_scalar(sp[:, g, :], pA[:, g, :], ba_sb[:, g:g + 1], GATE_FLOOR,
                                                ALU.add, ALU.max).then_inc(z_done, 1)

                def scan(b, p):
                    dve.wait_ge(sp_done, b + 1)
                    at_least(dve, lc_raw, G * b)
                    nc.vector.tensor_tensor_scan(lsum[:].rearrange(flat), keep[:].rearrange(flat),
                                                 sp[:].rearrange(flat), 0.0, ALU.mult, ALU.add).then_inc(l_done, 1)

                def centre(b, p):
                    dve.wait_ge(l_done, b + 1)
                    at_least(dve, ek_done, b)
                    at_least(dve, rng_done, b)
                    for g in range(G):
                        nc.vector.tensor_scalar(lc[:, g, :], lsum[:, g, :], lsum[:, g, P - 1:P], DECAY_LIMIT,
                                                ALU.subtract, ALU.min).then_inc(lc_raw, 1)
                    dve.wait_ge(lc_raw, G * (b + 1))
                    nc.vector.tensor_scalar(lc[:], lc[:], -DECAY_LIMIT, None, ALU.max).then_inc(lc_done, 1)

                def decay_q(b, p):
                    dve.wait_ge(q_ready, b + 1)
                    dve.wait_ge(eq_done, b + 1)
                    at_least(dve, at_ready, H * (b - 1))
                    nc.vector.tensor_tensor(qd[:, p], pQ, eq[:], ALU.mult).then_inc(qd_done, 1)

                def decay_k(b, p):
                    dve.wait_ge(sq_done, b + 1)
                    dve.wait_ge(ek_done, b + 1)
                    nc.vector.tensor_tensor(kd[:, p], pA[:], ek[:], ALU.mult).then_inc(kd_done, 1)

                def note_range(b, p):
                    dve.wait_ge(lc_done, b + 1)
                    nc.vector.tensor_copy(rng_sb[:, bass.ds(b, 1), :, :].rearrange("p a g e -> p (a g) e"),
                                          lc[:, :, 0:T:T - 1]).then_inc(rng_done, 1)

                def scale_v(b, p):
                    dve.wait_ge(ss_ready, b + 1)
                    at_least(dve, rn_done, 2 * b)
                    nc.vector.tensor_scalar(ss[:], pSS, NORM_EPS ** 2, None, ALU.max).then_inc(ss_done, 1)
                    dve.wait_ge(rn_done, 2 * b + 2)
                    dve.wait_ge(v_ready, b + 1)
                    at_least(dve, av_done, H * (b - 1))
                    nc.vector.tensor_tensor(vs[:, p].rearrange("p n (h d) -> p (n h) d", h=H),
                                            pB[:, :].rearrange("p (m d) -> p m d", d=DH),
                                            rn[:].rearrange("p n h -> p (n h)").unsqueeze(2).to_broadcast([P, TPB * H, DH]),
                                            ALU.mult).then_inc(vs_done, 1)

                def mask(b, h):
                    dve.wait_ge(at_ready, H * b + h + 1)
                    at_least(dve, av_done, H * b + h - 3)
                    nc.vector.tensor_tensor(am[:, h % 4, :], pAT[h % 2][:, 0:3 * P], causal[:],
                                            ALU.mult).then_inc(masked, 1)

                def residual(b):
                    dve.wait_ge(y_ready, b + 1)
                    nc.vector.scalar_tensor_tensor(y_sb[:, bass.ds(TPB * b, TPB), :], x_sb[:, bass.ds(TPB * b, TPB), :],
                                                   2.0, pY, ALU.mult, ALU.add).then_inc(y_done, 1)

                def step(i, p):
                    between = {-1: [gate_logits], 1: [scan], 2: [centre],
                               4: [decay_q], 5: [decay_k], 7: [note_range, scale_v]}
                    for h in range(-1, H):
                        if h >= 0:
                            mask(i, h)
                        if not is_last(i):
                            for stage_of_next in between.get(h, []):
                                stage_of_next(i + 1, 1 - p)
                    residual(i)

                statistics(0)
                statistics(1)
                normalise(0)
                statistics(2)
                normalise(1)
                dve.wait_ge(s_affine, 16 * 3)
                gate_logits(0, 0)
                statistics(3)
                dve.wait_ge(s_const, CONSTS)
                scan(0, 0)
                centre(0, 0)
                normalise(2)
                decay_q(0, 0)
                decay_k(0, 0)
                normalise(3)
                note_range(0, 0)
                scale_v(0, 0)
                rows(dve, step)

                dve.wait_ge(rng_done, B)
                nc.vector.tensor_tensor(rng_sb[:], rng_sb[:], rng_sb[:], ALU.mult).then_inc(s_fl, 1)
                dve.wait_ge(s_fl, 1)
                nc.vector.tensor_scalar(rng_sb[:], rng_sb[:], DECAY_LIMIT ** 2, None, ALU.is_lt).then_inc(s_fl, 1)
                dve.wait_ge(s_fl, 2)
                nc.vector.tensor_reduce(flag_f[:, 0:1], rng_sb[:].rearrange("p b g e -> p (b g e)"), AXIS.X,
                                        ALU.min).then_inc(s_fl, 1)

        with nc.Block() as block, ExitStack() as c2:
            pF = c2.enter_context(nc.psum_tensor("pF", [P, 512], F32))

            @block.tensor
            def _(pe):
                pe.wait_ge(s_fl, 3)
                nc.tensor.matmul(pF[0:1, 0:1], flag_f[:, 0:1], ones_col[:], start=True, stop=True).then_inc(s_flag_sum, 1)

            @block.vector
            def _(dve):
                dve.wait_ge(s_flag_sum, 1)
                nc.vector.tensor_copy(flag_i[0:1, :], pF[0:1, 0:1]).then_inc(s_flag, 1)

        with nc.Block() as block, ExitStack() as c3:
            def sb3(name, shape):
                return c3.enter_context(nc.sbuf_tensor(name, shape, F32))

            g_a = sb3("g_a", [P, T])
            g_k2 = sb3("g_k2", [P, T])
            g_q = sb3("g_q", [P, T])
            g_v = sb3("g_v", [P, T])
            g_n = sb3("g_n", [P, T])
            g_k = sb3("g_k", [P, T])
            g_kv, g_s, g_qs = sb3("g_kv", [P, T]), sb3("g_s", [P, T]), sb3("g_qs", [P, T])
            g_o = sb3("g_o", [P, G, T])
            same_head = sb3("same_head", [P, P])
            spread = sb3("spread", [P, HG, DH])
            place = sb3("place", [P, P])
            window = sb3("window", [P, 3 * DH])
            pz, pk, pq, pv, pn, pb, po, py = (c3.enter_context(nc.psum_tensor(f"g_p{n}", [P, 512], F32))
                                              for n in "zkqvnboy")

            g_const, g_proj, g_act, g_ss = sem("g_const"), sem("g_proj"), sem("g_act"), sem("g_ss")
            g_clamped, g_norm, g_in = sem("g_clamped"), sem("g_norm"), sem("g_in")
            g_sel, g_row, g_kv_done, g_s_done = sem("g_sel"), sem("g_row"), sem("g_kv_done"), sem("g_s_done")
            g_qs_done, g_summed, g_out = sem("g_qs_done"), sem("g_summed"), sem("g_out")
            g_y, g_y_done, g_z = sem("g_y"), sem("g_y_done"), sem("g_z")

            def out_of_range(eng):
                eng.wait_ge(s_flag, 1)
                return eng.If(eng.value_load(flag_i[0:1, 0:1]) < P)

            @block.gpsimd
            def _(pool):
                with out_of_range(pool):
                    nc.gpsimd.memset(same_head[:], 0.0).then_inc(g_const, 1)
                    nc.gpsimd.memset(window[:], 0.0).then_inc(g_const, 1)
                    pool.wait_ge(g_const, 2)
                    for hh in range(HG):
                        r = slice(hh * DH, hh * DH + DH)
                        nc.gpsimd.memset(same_head[r, r], 1.0).then_inc(g_const, 1)
                        nc.gpsimd.memset(window[r, DH * (1 + hh):DH * (1 + hh) + 1], 1.0).then_inc(g_const, 1)

            @block.tensor
            def _(pe):
                with out_of_range(pe):
                    pe.wait_ge(g_const, 2 + 2 * HG)
                    with pe.Fori(0, B) as b:
                        for g in range(G):
                            n = G * b + g
                            for dst, w in ((pz, wa_sb), (pk, wk_sb), (pq, wq_sb), (pv, wv_sb)):
                                mm = nc.tensor.matmul(dst[:, 0:T], w[:, g * P:(g + 1) * P], xnT[:, bass.ds(b * T, T)],
                                                      start=True, stop=True)
                            mm.then_inc(g_proj, 1)
                            pe.wait_ge(g_act, 4 * (n + 1))
                            nc.tensor.matmul(pn[:, 0:T], same_head[:], g_k2[:], start=True, stop=True).then_inc(g_ss, 1)
                            pe.wait_ge(g_in, n + 1)

                            def column(i, start, stop):
                                m = DH * n + i
                                pe.wait_ge(g_sel, 2 * (m + 1))
                                nc.tensor.matmul(pb[:, 0:T], spread[:].rearrange("p h d -> p (h d)"), g_v[:],
                                                 start=True, stop=True).then_inc(g_row, 1)
                                pe.wait_ge(g_qs_done, m + 1)
                                nc.tensor.matmul(po[:, 0:T], place[:], g_qs[:], start=start, stop=stop,
                                                 skip_group_check=True).then_inc(g_summed, 1)

                            column(0, True, False)
                            with pe.Fori(1, DH - 1) as i:
                                column(i, False, False)
                            column(DH - 1, False, True)
                            pe.wait_ge(g_out, n + 1)
                        for t in range(TPB):
                            for g in range(G):
                                mm = nc.tensor.matmul(py[:, t * D:(t + 1) * D], g_o[:, g, t * P:(t + 1) * P],
                                                      wo_sb[:, g, :], start=g == 0, stop=g == G - 1)
                        mm.then_inc(g_y, 1)
                        pe.wait_ge(g_y_done, b + 1)

            @block.scalar
            def _(act):
                with out_of_range(act):
                    with act.Fori(0, B) as b:
                        for g in range(G):
                            n = G * b + g
                            act.wait_ge(g_proj, n + 1)
                            act.wait_ge(g_z, n + 1)
                            nc.scalar.activation(g_a[:], g_a[:], ACT.Exp, scale=-1.0).then_inc(g_act, 1)
                            nc.scalar.activation(g_k2[:], pk[:, 0:T], ACT.Square).then_inc(g_act, 1)
                            nc.scalar.copy(g_q[:], pq[:, 0:T]).then_inc(g_act, 1)
                            nc.scalar.copy(g_v[:], pv[:, 0:T]).then_inc(g_act, 1)
                            act.wait_ge(g_clamped, n + 1)
                            nc.scalar.activation(g_n[:], g_n[:], ACT.Sqrt).then_inc(g_norm, 1)

            @block.vector
            def _(dve):
                with out_of_range(dve):
                    dve.wait_ge(g_const, 2 + 2 * HG)
                    with dve.Fori(0, B) as b:
                        for g in range(G):
                            n = G * b + g
                            dve.wait_ge(g_proj, n + 1)
                            nc.vector.tensor_scalar(g_a[:], pz[:, 0:T], ba_sb[:, g:g + 1], SIGMOID_FLOOR,
                                                    ALU.add, ALU.max).then_inc(g_z, 1)
                            dve.wait_ge(g_act, 4 * (n + 1))
                            nc.vector.tensor_scalar(g_a[:], g_a[:], 1.0, None, ALU.add).then_inc(g_norm, 1)
                            dve.wait_ge(g_ss, n + 1)
                            nc.vector.tensor_scalar(g_n[:], pn[:, 0:T], NORM_EPS ** 2, None, ALU.max).then_inc(g_clamped, 1)
                            dve.wait_ge(g_norm, 4 * n + 2)
                            nc.vector.reciprocal(g_a[:], g_a[:]).then_inc(g_norm, 1)
                            nc.vector.reciprocal(g_n[:], g_n[:]).then_inc(g_norm, 1)
                            dve.wait_ge(g_norm, 4 * (n + 1))
                            nc.vector.tensor_tensor(g_k[:], pk[:, 0:T], g_n[:], ALU.mult).then_inc(g_in, 1)
                            with dve.Fori(0, DH) as i:
                                m = DH * n + i
                                dve.wait_ge(g_in, n + 1)
                                unit = ident[:].rearrange("p (h d) -> p h d", h=HG)[:, :, bass.ds(i, 1)]
                                nc.vector.tensor_scalar(spread[:], unit.to_broadcast([P, HG, DH]), 1.0, None,
                                                        ALU.mult).then_inc(g_sel, 1)
                                nc.vector.tensor_scalar(place[:], window[:, bass.ds(DH - i, P)], 1.0, None,
                                                        ALU.mult).then_inc(g_sel, 1)
                                dve.wait_ge(g_row, m + 1)
                                nc.vector.tensor_tensor(g_kv[:], g_k[:], pb[:, 0:T], ALU.mult).then_inc(g_kv_done, 1)
                                dve.wait_ge(g_kv_done, m + 1)
                                nc.vector.tensor_tensor_scan(g_s[:], g_a[:], g_kv[:], 0.0, ALU.mult,
                                                             ALU.add).then_inc(g_s_done, 1)
                                dve.wait_ge(g_s_done, m + 1)
                                nc.vector.tensor_tensor(g_qs[:], g_s[:], g_q[:], ALU.mult).then_inc(g_qs_done, 1)
                                dve.wait_ge(g_summed, m + 1)
                            dve.wait_ge(g_summed, DH * (n + 1))
                            nc.vector.tensor_copy(g_o[:, g, :], po[:, 0:T]).then_inc(g_out, 1)
                        dve.wait_ge(g_y, b + 1)
                        nc.vector.scalar_tensor_tensor(y_sb[:, bass.ds(TPB * b, TPB), :], x_sb[:, bass.ds(TPB * b, TPB), :],
                                                       2.0, py[:, 0:TPB * D].rearrange("p (n d) -> p n d", n=TPB),
                                                       ALU.mult, ALU.add).then_inc(g_y_done, 1)

        att.close()
        stage = sb("stage", [P, TOPK, NTILES, ROW])
        w1_hi = sb("w1_hi", [P, E, F], F32R)
        w3_hi = sb("w3_hi", [P, E, F], F32R)
        with nc.Block() as block, ExitStack() as c4:
            def sb4(name, shape, dt=F32):
                return c4.enter_context(nc.sbuf_tensor(name, shape, dt))

            TG = 8
            NG = NTILES // TG
            st = sb4("st", [P, NTILES, 6])
            mean, var, tmp, rs = (sb4(n, [P, NTILES]) for n in ("mean", "var", "tmp", "rs"))
            slot_i = sb4("slot_i", [P, TOPK, NTILES], I32)
            x1T = sb4("x1T", [P, TG * P])
            probs, pr2, tie, rank = (sb4(n, [P, TG, E]) for n in ("probs", "pr2", "tie", "rank"))
            both = sb4("both", [P, E, TG])
            chosen = sb4("chosen", [P, TOPK, TG, E])
            low, wsum, top = sb4("low", [P, TG]), sb4("wsum", [P, TG]), sb4("top", [P, TOPK, TG])
            slot_e, slot_f = sb4("slot_e", [P, TOPK, TG, E]), sb4("slot_f", [P, TOPK, TG])
            pT = [c4.enter_context(nc.psum_tensor(f"r_pT{i}", [P, 512], F32)) for i in range(2)]
            pL = [c4.enter_context(nc.psum_tensor(f"r_pL{i}", [P, 512], F32)) for i in range(2)]
            pR = c4.enter_context(nc.psum_tensor("r_pR", [P, 512], F32))
            upto, base = sb4("upto", [P, E, TG]), sb4("base", [P, E, TG])
            restart = sb4("restart", [P, E, TG])
            before = pR[:, 0:TG * E].rearrange("p (e t) -> p t e", t=TG)
            total = pR[:, TG * E:2 * TG * E]
            HALF = TG // 2

            def parts(n):
                es = slice(n * E // NG, (n + 1) * E // NG)
                return (w1_hi[:, es], w1_lo[:, es]), (w3_hi[:, es], w3_lo[:, es])


            m_bn, m_join, m_rs, m_x1, m_x1b = sem("m_bn"), sem("m_join"), sem("m_rs"), sem("m_x1"), sem("m_x1b")
            m_xt, m_x1T, m_logits, m_exp, m_route = sem("m_xt"), sem("m_x1T"), sem("m_logits"), sem("m_exp"), sem("m_route")
            m_both, m_ranks, m_slots = sem("m_both"), sem("m_ranks"), sem("m_slots")
            m_hi, m_lo, m_restart = sem("m_hi"), sem("m_lo"), sem("m_restart")
            ROUTE = 28

            def logits(n):
                return pL[n % 2][:, 0:TG * E].rearrange("p (t e) -> p t e", t=TG)

            @block.tensor
            def _(pe):
                def turn_x1(n):
                    for a in range(2):
                        pe.wait_ge(m_x1, TG * n + HALF * (a + 1))
                        at_least(pe, m_x1T, 2 * (n - 1) + a + 1)
                        for t in range(HALF):
                            mm = nc.tensor.transpose(pT[a][:, t * P:(t + 1) * P],
                                                     stage[:, 0, n * TG + a * HALF + t, 0:D], ident[:])
                        mm.then_inc(m_xt, 1)
                    pe.wait_ge(m_x1T, 2 * (n + 1))
                    for t in range(TG):
                        mm = nc.tensor.matmul(logits(n)[:, t, :], x1T[:, t * P:(t + 1) * P], wr_sb[:], start=True, stop=True)
                    mm.then_inc(m_logits, 1)

                pe.wait_ge(s_wr, 16)
                turn_x1(0)
                for n in range(NG):
                    if n + 1 < NG:
                        turn_x1(n + 1)
                    pe.wait_ge(m_both, n + 1)
                    one_hots = both[:].rearrange("p e t -> p (e t)")
                    nc.tensor.matmul(pR[:, 0:TG * E], earlier[:], one_hots, start=True, stop=True)
                    nc.tensor.matmul(pR[:, TG * E:2 * TG * E], all_ones[:], one_hots,
                                     start=True, stop=True).then_inc(m_ranks, 1)

            @block.scalar
            def _(act):
                load_table(EXP_LN_SET)

                def deviations(n):
                    tl = slice(n * TG, (n + 1) * TG)
                    act.wait_ge(m_join, 6 * (n + 1))
                    nc.scalar.activation(rs[:, tl], var[:, tl], ACT.Ln, bias=eps_sb[:, 0:1]).then_inc(m_rs, 1)
                    act.wait_ge(m_rs, 2 * n + 1)
                    nc.scalar.activation(rs[:, tl], rs[:, tl], ACT.Exp, scale=-0.5).then_inc(m_rs, 1)

                def copy_turned(n):
                    at_least(act, m_logits, n)
                    for a in range(2):
                        act.wait_ge(m_xt, 2 * n + a + 1)
                        nc.scalar.copy(x1T[:, a * HALF * P:(a + 1) * HALF * P], pT[a][:]).then_inc(m_x1T, 1)

                def second_rows(n):
                    tl = slice(n * TG, (n + 1) * TG)
                    nc.scalar.copy(stage[:, 1, tl, 0:D], stage[:, 0, tl, 0:D]).then_inc(m_x1b, 1)

                deviations(0)
                copy_turned(0)
                second_rows(0)
                act.wait_ge(s_wm, 48)
                for n in range(NG):
                    if n + 1 < NG:
                        deviations(n + 1)
                    act.wait_ge(m_route, ROUTE * n + 2)
                    nc.scalar.activation(probs[:], probs[:], ACT.Exp).then_inc(m_exp, 1)
                    if n + 1 < NG:
                        copy_turned(n + 1)
                    for high, whole in parts(n):
                        nc.scalar.copy(high, whole.bitcast(F32)).then_inc(m_hi, 1)
                    if n + 1 < NG:
                        second_rows(n + 1)

            @block.sync
            def _(sp):
                sp.wait_ge(m_pad, 1)
                for e in range(E):
                    row = sp.value_load(pad_i[0:1, e:e + 1], min_val=0, max_val=NROWS - P)
                    sp.dma_start(rows_d[bass.ds(row, P), :], empty[:]).then_inc(s_pads, 16)
                sp.wait_ge(s_pads, 16 * E)

            @block.gpsimd
            def _(pool):
                nc.gpsimd.memset(restart[:], 1.0).then_inc(m_restart, 1)
                pool.wait_ge(m_restart, 1)
                nc.gpsimd.memset(restart[:, :, 0:1], 0.0).then_inc(m_restart, 1)
                pool.wait_ge(s_fill, 16)
                for n in range(NG):
                    pool.wait_ge(m_slots, n + 1)
                    pool.sem_inc(s_turn, 1)
                    for t in range(n * TG, (n + 1) * TG):
                        for k in range(TOPK):
                            nc.gpsimd.indirect_dma_start(
                                out=rows_d[:, :], out_offset=bass.IndirectOffsetOnAxis(ap=slot_i[:, k, t:t + 1], axis=0),
                                in_=stage[:, k, t, :], in_offset=None).then_inc(s_sent, 16)
                pool.wait_ge(s_sent, 16 * TOPK * NTILES)

            @block.vector
            def _(dve):
                def normalise(n):
                    tl = slice(n * TG, (n + 1) * TG)
                    for t in range(n * TG, (n + 1) * TG):
                        nc.vector.bn_stats(st[:, t, :], y_sb[:, t, :]).then_inc(m_bn, 1)
                    dve.wait_ge(m_bn, TG * (n + 1))
                    join_halves(dve, st[:, tl], mean[:, tl], var[:, tl], tmp[:, tl], m_join, 6 * n)
                    dve.wait_ge(m_rs, 2 * (n + 1))
                    for t in range(n * TG, (n + 1) * TG):
                        nc.vector.tensor_scalar(stage[:, 0, t, 0:D], y_sb[:, t, :], mean[:, t:t + 1], rs[:, t:t + 1],
                                                ALU.subtract, ALU.mult).then_inc(m_x1, 1)

                def route(n):
                    tl = slice(n * TG, (n + 1) * TG)
                    did = [0]

                    def then(ins):
                        did[0] += 1
                        ins.then_inc(m_route, 1)
                        dve.wait_ge(m_route, ROUTE * n + did[0])

                    def over(v):
                        return v.unsqueeze(2).to_broadcast([P, TG, E])

                    idx = iota8[:].unsqueeze(1).to_broadcast([P, TG, E])
                    dve.wait_ge(m_logits, n + 1)
                    then(nc.vector.tensor_reduce(low[:], logits(n), AXIS.X, ALU.max))
                    then(nc.vector.tensor_tensor(probs[:], logits(n), over(low[:]), ALU.subtract))
                    dve.wait_ge(m_exp, n + 1)
                    then(nc.vector.tensor_reduce(low[:], probs[:], AXIS.X, ALU.add))
                    then(nc.vector.reciprocal(low[:], low[:]))
                    then(nc.vector.tensor_tensor(probs[:], probs[:], over(low[:]), ALU.mult))
                    cur = probs
                    for k in range(TOPK):
                        then(nc.vector.tensor_reduce(top[:, k, :], cur[:], AXIS.X, ALU.max))
                        then(nc.vector.tensor_tensor(tie[:], cur[:], over(top[:, k, :]), ALU.is_equal))
                        then(nc.vector.tensor_tensor(tie[:], tie[:], idx, ALU.mult))
                        then(nc.vector.tensor_reduce(low[:], tie[:], AXIS.X, ALU.min))
                        then(nc.vector.tensor_tensor(chosen[:, k], idx, over(low[:]), ALU.is_equal))
                        if k == 0:
                            then(nc.vector.scalar_tensor_tensor(pr2[:], chosen[:, 0], -2.0, probs[:], ALU.mult, ALU.add))
                            cur = pr2
                    nc.vector.tensor_tensor(both[:].rearrange("p e t -> p t e"), chosen[:, 0], chosen[:, 1], ALU.add).then_inc(m_both, 1)
                    then(nc.vector.tensor_tensor(wsum[:], top[:, 0, :], top[:, 1, :], ALU.add))
                    then(nc.vector.reciprocal(wsum[:], wsum[:]))
                    then(nc.vector.tensor_tensor(stage[:, :, tl, D], top[:], wsum[:].unsqueeze(1).to_broadcast([P, TOPK, TG]),
                                                 ALU.mult))
                    then(nc.vector.tensor_copy(stage[:, :, tl, D + 1], made_to[:, :, tl]))
                    for c, (high, whole) in enumerate(parts(n)):
                        dve.wait_ge(m_hi, 2 * n + c + 1)
                        nc.vector.tensor_tensor(whole, whole.bitcast(F32), high.bitcast(F32), ALU.subtract).then_inc(m_lo, 1)
                    dve.wait_ge(m_ranks, n + 1)
                    then(nc.vector.tensor_tensor_scan(upto[:].rearrange("p e t -> p (e t)"), restart[:].rearrange("p e t -> p (e t)"), total, 0.0, ALU.mult, ALU.add))
                    then(nc.vector.tensor_tensor(base[:].rearrange("p e t -> p (e t)"), upto[:].rearrange("p e t -> p (e t)"), total, ALU.subtract))
                    then(nc.vector.tensor_tensor(base[:], base[:], next_row[:].unsqueeze(2).to_broadcast([P, E, TG]), ALU.add))
                    then(nc.vector.tensor_tensor(rank[:], before, base[:].rearrange("p e t -> p t e"), ALU.add))
                    then(nc.vector.tensor_tensor(next_row[:], next_row[:], upto[:, :, TG - 1], ALU.add))
                    for k in range(TOPK):
                        then(nc.vector.tensor_tensor(slot_e[:, k], chosen[:, k], rank[:], ALU.mult))
                    then(nc.vector.tensor_reduce(slot_f[:].rearrange("p k t -> p (k t)"),
                                                 slot_e[:].rearrange("p k t e -> p (k t) e"), AXIS.X, ALU.add))
                    assert did[0] == ROUTE, did
                    dve.wait_ge(m_x1b, n + 1)
                    nc.vector.tensor_copy(slot_i[:, :, tl], slot_f[:]).then_inc(m_slots, 1)

                dve.wait_ge(s_const, CONSTS)
                nc.vector.tensor_copy(next_row[:], first_row[:]).then_inc(m_first, 1)
                dve.wait_ge(m_first, 1)
                dve.wait_ge(m_restart, 2)
                normalise(0)
                for n in range(NG):
                    if n + 1 < NG:
                        normalise(n + 1)
                    route(n)
                nc.vector.tensor_copy(pad_i[:], next_row[:]).then_inc(m_pad, 1)

                done = [0]

                def then(ins):
                    done[0] += 1
                    ins.then_inc(m_table, 1)
                    dve.wait_ge(m_table, done[0])

                then(nc.vector.tensor_tensor(count[:], next_row[:], first_row[:], ALU.subtract))
                then(nc.vector.tensor_tensor(full[:], count[:].unsqueeze(2).to_broadcast([P, E, NTILES]),
                                             tile_edge[:, 0:NTILES].unsqueeze(1).to_broadcast([P, E, NTILES]), ALU.is_gt))
                then(nc.vector.tensor_reduce(ntile[:], full[:], AXIS.X, ALU.add))
                then(nc.vector.tensor_tensor_scan(tiles_to[:], ones8[:], ntile[:], 0.0, ALU.mult, ALU.add))
                then(nc.vector.tensor_tensor(tiles_from[:], tiles_to[:], ntile[:], ALU.subtract))
                num = tile_no[:].unsqueeze(2).to_broadcast([P, NSLOT, E])

                def each(v):
                    return v.unsqueeze(1).to_broadcast([P, NSLOT, E])

                then(nc.vector.tensor_tensor(mine[:], num, each(tiles_from[:]), ALU.is_ge))
                then(nc.vector.tensor_tensor(work[:], num, each(tiles_to[:]), ALU.is_ge))
                then(nc.vector.tensor_tensor(mine[:], mine[:], work[:], ALU.subtract))
                then(nc.vector.tensor_tensor(work[:], mine[:], each(expert_no[:]), ALU.mult))
                then(nc.vector.tensor_reduce(slot_tab[:], work[:], AXIS.X, ALU.add))
                then(nc.vector.tensor_copy(expert_i[:], slot_tab[:]))
                then(nc.vector.tensor_tensor(work[:], num, each(tiles_from[:]), ALU.subtract))
                then(nc.vector.tensor_scalar(work[:], work[:], float(P), None, ALU.mult))
                then(nc.vector.tensor_tensor(work[:], work[:], each(first_row[:]), ALU.add))
                then(nc.vector.tensor_scalar(work[:], work[:], float(EMPTY_ROW), None, ALU.subtract))
                then(nc.vector.tensor_tensor(work[:], work[:], mine[:], ALU.mult))
                then(nc.vector.tensor_reduce(slot_tab[:], work[:], AXIS.X, ALU.add))
                then(nc.vector.tensor_scalar(slot_tab[:], slot_tab[:], float(EMPTY_ROW), None, ALU.add))
                then(nc.vector.tensor_copy(row_i[:], slot_tab[:]))

        with nc.Block() as block, ExitStack() as c5:
            def sb5(name, shape, dt=F32):
                return c5.enter_context(nc.sbuf_tensor(name, shape, dt))

            def ps5(name, shape):
                return c5.enter_context(nc.psum_tensor(name, shape, F32))

            xt = sb5("xt", [P, 4, ROW])
            x_hi, x_lo = sb5("x_hi", [P, 2, P], F32R), sb5("x_lo", [P, 2, P], F32R)
            sg = sb5("sg", [P, 2, F])
            hid = sb5("hid", [P, 2, F])
            hT = sb5("hT", [P, 2, FC, P])
            yt = sb5("yt", [P, 4, D])
            to_f = sb5("to_f", [P, 4])
            to_i = sb5("to_i", [P, 4], I32)
            pX = ps5("pX", [P, 512])
            pG = [ps5(f"pG{i}", [P, F]) for i in range(2)]
            pU = [ps5(f"pU{i}", [P, F]) for i in range(2)]
            pH = ps5("pH", [P, FC, P])
            pD = [ps5(f"pD{i}", [P, 512]) for i in range(2)]

            t_load = [sem(f"t_load{i}") for i in range(4)]
            t_turned, t_x_hi, t_x_lo, t_gate, t_up = sem("t_turned"), sem("t_x_hi"), sem("t_x_lo"), sem("t_gate"), sem("t_up")
            t_silu, t_hid, t_ht, t_hT = sem("t_silu"), sem("t_hid"), sem("t_ht"), sem("t_hT")
            t_down, t_y, t_to = sem("t_down"), sem("t_y"), sem("t_to")
            t_made = [sem(f"t_made{r}") for r in range(4)]

            def tiles(eng, step):
                for j in range(4):
                    step(j, j, 1)
                with eng.Fori(1, NSLOT // 4 - 1) as q:
                    for r in range(4):
                        step(4 * q + r, r, q + 1)
                for r in range(4):
                    step(NSLOT - 4 + r, r, NSLOT // 4)

            def tile(j, r, turn, by):
                if isinstance(j, int) and j + by >= NSLOT:
                    return None
                return j + by, (r + by) % 4, turn + (r + by) // 4

            @block.sync
            def _(sp):
                sp.wait_ge(m_table, TABLE)

                def step(j, r, turn):
                    row = sp.value_load(row_i[0:1, bass.ds(j, 1)], min_val=0, max_val=NROWS - P)
                    at_least(sp, t_y, 2 * (j - 3))
                    sp.dma_start(xt[:, r, :], rows_d[bass.ds(row, P), :]).then_inc(t_load[r], 16)

                tiles(sp, step)

            @block.tensor
            def _(pe):
                pe.wait_ge(m_table, TABLE)
                pe.wait_ge(m_lo, 2 * (NTILES // 8))

                def expert(j):
                    return pe.value_load(expert_i[0:1, bass.ds(j, 1)], min_val=0, max_val=E - 1)

                def weights(w, e):
                    return w[:, bass.ds(e, 1), :].rearrange("p a f -> p (a f)")

                def product(out, x_parts, w_parts):
                    for k, (a, b) in enumerate(((0, 0), (0, 1), (1, 0))):
                        mm = nc.tensor.matmul(out, x_parts[a], w_parts[b], start=k == 0, stop=k == 2)
                    return mm

                def turn_rows(j, r, turn):
                    pe.wait_ge(t_load[r], 16 * turn)
                    at_least(pe, t_x_lo, j)
                    nc.tensor.transpose(pX[:, 0:P], xt[:, r, 0:D], ident[:]).then_inc(t_turned, 1)

                def gate_up(j, r, e):
                    p = r % 2
                    x_parts = x_hi[:, p, :], x_lo[:, p, :]
                    pe.wait_ge(t_x_lo, j + 1)
                    at_least(pe, t_silu, j - 1)
                    product(pG[p][:], x_parts, (weights(w1_hi, e), weights(w1_lo, e))).then_inc(t_gate, 1)
                    at_least(pe, t_hid, j - 1)
                    product(pU[p][:], x_parts, (weights(w3_hi, e), weights(w3_lo, e))).then_inc(t_up, 1)

                def turn_hidden(j, r):
                    pe.wait_ge(t_hid, j + 1)
                    at_least(pe, t_hT, j)
                    for c in range(FC):
                        mm = nc.tensor.transpose(pH[:, c, :], hid[:, r % 2, c * P:(c + 1) * P], ident[:])
                    mm.then_inc(t_ht, 1)

                def down(j, r, e):
                    pe.wait_ge(t_hT, j + 1)
                    at_least(pe, t_y, 2 * (j - 1))
                    for c in range(FC):
                        mm = nc.tensor.matmul(pD[r % 2][:, 0:D], hT[:, r % 2, c, :],
                                              w2_sb[:, bass.ds(e, 1), c, :].rearrange("p a d -> p (a d)"),
                                              start=c == 0, stop=c == FC - 1)
                    mm.then_inc(t_down, 1)

                turn_rows(0, 0, 1)
                turn_rows(1, 1, 1)
                gate_up(0, 0, expert(0))
                of_tile = {}

                def step(j, r, turn):
                    one, two = (tile(j, r, turn, by) for by in (1, 2))
                    if r == 0:
                        of_tile["next"] = expert(j + 1)
                    turn_hidden(j, r)
                    if one:
                        gate_up(*one[:2], of_tile["next"])
                    if two:
                        turn_rows(*two)
                    after = expert(two[0]) if two and r < 3 else None
                    if r == 0:
                        of_tile["this"] = expert(j)
                    down(j, r, of_tile["this"])
                    of_tile["this"], of_tile["next"] = of_tile["next"], after

                tiles(pe, step)

            @block.scalar
            def _(act):
                def high_x(j, r):
                    act.wait_ge(t_turned, j + 1)
                    at_least(act, t_up, j - 1)
                    nc.scalar.copy(x_hi[:, r % 2, :], pX[:, 0:P]).then_inc(t_x_hi, 1)

                def silu(j, r):
                    act.wait_ge(t_gate, j + 1)
                    at_least(act, t_hid, j - 1)
                    nc.scalar.activation(sg[:, r % 2, :], pG[r % 2][:], ACT.Silu).then_inc(t_silu, 1)

                def copy_hidden(j, r):
                    act.wait_ge(t_ht, j + 1)
                    at_least(act, t_down, j - 1)
                    nc.scalar.copy(hT[:, r % 2], pH[:]).then_inc(t_hT, 1)

                high_x(0, 0)
                high_x(1, 1)
                silu(0, 0)

                def step(j, r, turn):
                    one, two = (tile(j, r, turn, by) for by in (1, 2))
                    copy_hidden(j, r)
                    if one:
                        silu(*one[:2])
                    if two:
                        high_x(*two[:2])

                tiles(act, step)

            @block.vector
            def _(dve):
                def low_x(j, r):
                    dve.wait_ge(t_x_hi, j + 1)
                    at_least(dve, t_up, j - 1)
                    nc.vector.tensor_tensor(x_lo[:, r % 2, :], pX[:, 0:P], x_hi[:, r % 2, :].bitcast(F32),
                                            ALU.subtract).then_inc(t_x_lo, 1)

                def hidden(j, r):
                    p = r % 2
                    dve.wait_ge(t_silu, j + 1)
                    dve.wait_ge(t_up, j + 1)
                    at_least(dve, t_ht, j - 1)
                    nc.vector.tensor_tensor(hid[:, p, :], pU[p][:], sg[:, p, :], ALU.mult).then_inc(t_hid, 1)

                def scaled(j, r, turn):
                    dve.wait_ge(t_load[r], 16 * turn)
                    at_least(dve, t_made[r], 16 * (turn - 1))
                    nc.vector.tensor_scalar(to_f[:, r:r + 1], xt[:, r, D + 1:D + 2], float(TOPK * NT), tile_edge[:, bass.ds(j, 1)],
                                            ALU.is_ge, ALU.mult).then_inc(t_to, 1)
                    dve.wait_ge(t_to, j + 1)
                    nc.vector.tensor_tensor(to_i[:, r:r + 1], to_f[:, r:r + 1], xt[:, r, D + 1:D + 2],
                                            ALU.add).then_inc(t_y, 1)
                    dve.wait_ge(t_down, j + 1)
                    nc.vector.tensor_scalar(yt[:, r, :], pD[r % 2][:, 0:D], xt[:, r, D:D + 1], None, ALU.mult).then_inc(t_y, 1)

                low_x(0, 0)
                low_x(1, 1)
                hidden(0, 0)

                def step(j, r, turn):
                    one, two = (tile(j, r, turn, by) for by in (1, 2))
                    if one:
                        hidden(*one[:2])
                    if two:
                        low_x(*two[:2])
                    scaled(j, r, turn)

                tiles(dve, step)

            @block.gpsimd
            def _(pool):
                def step(j, r, turn):
                    p = r % 2
                    pool.wait_ge(t_y, 2 * (j + 1))
                    pool.sem_inc(s_turn, 1)
                    nc.gpsimd.indirect_dma_start(
                        out=made_d[:, :], out_offset=bass.IndirectOffsetOnAxis(ap=to_i[:, r:r + 1], axis=0),
                        in_=yt[:, r, :], in_offset=None).then_inc(t_made[r], 16)

                tiles(pool, step)
                for r in range(4):
                    pool.wait_ge(t_made[r], 16 * (NSLOT // 4))

        with nc.Block() as block, ExitStack() as c6:
            def sb6(name, shape, dt=F32):
                return c6.enter_context(nc.sbuf_tensor(name, shape, dt))

            made = sb6("made", [P, TOPK, NTILES, D])
            fo = sb6("fo", [P, 4, TB, D])
            fst = sb6("fst", [P, NTILES, 6])
            fmean, fvar, ftmp, frs, fshift = (sb6(n, [P, NTILES]) for n in ("fmean", "fvar", "ftmp", "frs", "fshift"))
            f_load = [sem(f"f_load{n}") for n in range(NBLK)]
            f_made, f_x, f_bn, f_join = sem("f_made"), sem("f_x"), sem("f_bn"), sem("f_join")
            f_rs, f_shift, f_fo = sem("f_rs"), sem("f_shift"), sem("f_fo")
            f_out = [sem(f"f_out{k}") for k in range(4)]

            def of_block(n):
                return slice(n * TB, (n + 1) * TB)

            @block.sync
            def _(sp):
                made_v = made_d[0:TOPK * NT, :].rearrange("(k n p) d -> p k n d", p=P, k=TOPK)
                for n in range(NBLK):
                    for k in range(TOPK):
                        sp.dma_start(made[:, k, n * TB:(n + 1) * TB, :],
                                     made_v[:, k, n * TB:(n + 1) * TB, :]).then_inc(f_load[n], 16)
                for n in range(NBLK):
                    sp.wait_ge(f_fo, TB * (n + 1))
                    sp.dma_start(out_d[:, n * TB:(n + 1) * TB, :], fo[:, n % 4]).then_inc(f_out[n % 4], 16)
                for k in range(4):
                    sp.wait_ge(f_out[k], 16 * (NBLK // 4))

            @block.gpsimd
            def _(pool):
                for n in range(NBLK):
                    pool.wait_ge(f_load[n], 16 * TOPK)
                    nc.gpsimd.tensor_tensor(made[:, 0, of_block(n), :], made[:, 0, of_block(n), :],
                                            made[:, 1, of_block(n), :], ALU.add).then_inc(f_made, 1)

            @block.scalar
            def _(act):
                load_table(EXP_LN_SET)

                def deviations(n):
                    act.wait_ge(f_join, 6 * (n + 1))
                    nc.scalar.activation(frs[:, of_block(n)], fvar[:, of_block(n)], ACT.Ln, bias=eps_sb[:, 0:1]).then_inc(f_rs, 1)
                    act.wait_ge(f_rs, 2 * n + 1)
                    nc.scalar.activation(frs[:, of_block(n)], frs[:, of_block(n)], ACT.Exp, scale=-0.5).then_inc(f_rs, 1)

                deviations(0)
                for n in range(NBLK):
                    if n + 1 < NBLK:
                        deviations(n + 1)
                    act.wait_ge(f_shift, n + 1)
                    at_least(act, f_out[n % 4], 16 * (n // 4))
                    for t in range(TB):
                        i = n * TB + t
                        nc.scalar.activation(fo[:, n % 4, t, :], made[:, 0, i, :], ACT.Identity,
                                             scale=frs[:, i:i + 1], bias=fshift[:, i:i + 1]).then_inc(f_fo, 1)

            @block.vector
            def _(dve):
                def statistics(n):
                    blk = of_block(n)
                    dve.wait_ge(f_made, n + 1)
                    nc.vector.tensor_tensor(made[:, 0, blk, :], made[:, 0, blk, :], stage[:, 0, blk, 0:D],
                                            ALU.add).then_inc(f_x, 1)
                    dve.wait_ge(f_x, n + 1)
                    for t in range(n * TB, (n + 1) * TB):
                        nc.vector.bn_stats(fst[:, t, :], made[:, 0, t, :]).then_inc(f_bn, 1)
                    dve.wait_ge(f_bn, TB * (n + 1))
                    join_halves(dve, fst[:, blk], fmean[:, blk], fvar[:, blk], ftmp[:, blk], f_join, 6 * n)

                statistics(0)
                for n in range(NBLK):
                    if n + 1 < NBLK:
                        statistics(n + 1)
                    dve.wait_ge(f_rs, 2 * (n + 1))
                    blk = of_block(n)
                    nc.vector.scalar_tensor_tensor(fshift[:, blk], fmean[:, blk], -1.0, frs[:, blk],
                                                   ALU.mult, ALU.mult).then_inc(f_shift, 1)


_INS = ["L0_attn_x", "L0_attn_Wq", "L0_attn_Wk", "L0_attn_Wv", "L0_attn_Wa", "L0_attn_ba", "L0_attn_Wo",
        "L0_attn_gamma", "L0_attn_beta", "L0_ffn_Wr", "L0_ffn_W1", "L0_ffn_W2", "L0_ffn_W3"]


def kernel(**inputs):
    import numpy as np
    import concourse.bacc as bacc
    from concourse import mybir as mb
    from concourse.bass_utils import run_bass_kernel_spmd

    nc = bacc.Bacc("TRN2", target_bir_lowering=False, num_devices=1)
    arrays, args = {}, []
    for name in _INS:
        a = np.asarray(inputs[name])
        if name == "L0_ffn_Wr":
            a = a.T
        if name == "L0_attn_ba":
            a = a.reshape(-1, 128).T
        a = np.ascontiguousarray(a)
        arrays[f"in_{name}"] = a
        args.append(nc.dram_tensor(f"in_{name}", a.shape, mb.dt.from_np(a.dtype), kind="ExternalInput").ap())
    shape = tuple(inputs["L0_attn_x"].shape)
    out = nc.dram_tensor("out_0", shape, mb.dt.float32, kind="ExternalOutput").ap()
    build(nc, *args, out)
    r = run_bass_kernel_spmd(nc, [arrays], core_ids=[0])
    return r.results[0]["out_0"]
```
